# Optimizing a Trainium2 kernel written in Bass

```python
import numpy as np
import jax
import jax.numpy as jnp

def _softmax(x, axis=-1):
    return jax.nn.softmax(x, axis=axis)

def _gelu(x):
    return jax.nn.gelu(x, approximate=True)

def _silu(x):
    return jax.nn.silu(x)

def _sigmoid(x):
    return jax.nn.sigmoid(x)

def _layernorm(x, axis=-1, eps=1e-05):
    m = jnp.mean(x, axis=axis, keepdims=True)
    v = jnp.var(x, axis=axis, keepdims=True)
    return (x - m) / jnp.sqrt(v + eps)

def _scatter_add(tgt, idx, src, axis=0):
    return tgt.at[idx].add(src)

def _segment_sum(src, seg, n):
    return jax.ops.segment_sum(src, seg, n)
kernel_name = 'mk_gnn_ffn_d2_gnn_r8_a9b782'

def setup_inputs(seed: int=0):
    np.random.seed(seed)
    _w = jnp.asarray

    def _rec_inputs():
        import jax
        import jax.numpy as jnp
        _gk = jax.random.key(seed)
        x = -8.776e-05 + 1 * jax.random.normal(jax.random.fold_in(_gk, 1), (6250, 256), jnp.float32)
        _s = jax.random.randint(jax.random.fold_in(_gk, 2), (100000,), 0, 6250, jnp.int32)
        _d = jax.random.randint(jax.random.fold_in(_gk, 3), (100000,), 0, 6250, jnp.int32)
        _loop = jnp.arange(6250, dtype=jnp.int32)
        src = jnp.concatenate([_s, _d, _loop])
        dst = jnp.concatenate([_d, _s, _loop])
        _o = jnp.argsort(dst, stable=True)
        src = src[_o]
        dst = dst[_o]
        edge_type_16 = jax.random.randint(jax.random.fold_in(_gk, 12), (206250,), 0, 16, jnp.int32)
        edge_weight = jax.random.uniform(jax.random.fold_in(_gk, 13), (206250,), jnp.float32, 0.0, 0.999999)
        edge_weight1 = jax.random.uniform(jax.random.fold_in(_gk, 14), (206250, 1), jnp.float32, 0.0, 0.999998)
        return (x, src, dst, edge_type_16, edge_weight, edge_weight1)
    x, src, dst, edge_type_16, edge_weight, edge_weight1 = _rec_inputs()

    def _L0_gnn_setup():
        import jax, jax.numpy as jnp
        import numpy as np
        N_NODES = 2500
        N_EDGES = 40000
        NUM_RELS = 16
        IN_FEAT = 256
        OUT_FEAT = 256
        key = jax.random.key(seed)
        k_h, k_w, k_n, k_s, k_d, k_r = jax.random.split(key, 6)
        h = jax.random.normal(k_h, (N_NODES, IN_FEAT), dtype=jnp.float32)
        weight = jax.random.normal(k_w, (NUM_RELS, IN_FEAT, OUT_FEAT), dtype=jnp.float32)
        norm = jax.random.uniform(k_n, (N_EDGES, 1), dtype=jnp.float32)
        src = jax.random.randint(k_s, (N_EDGES,), 0, N_NODES, dtype=jnp.int32)
        dst = jax.random.randint(k_d, (N_EDGES,), 0, N_NODES, dtype=jnp.int32)
        rel_type = jax.random.randint(k_r, (N_EDGES,), 0, NUM_RELS, dtype=jnp.int32)
        return {'h': h, 'weight': weight, 'norm': norm, 'src': src, 'dst': dst, 'rel_type': rel_type}
    _L0_gnn_all = _L0_gnn_setup()
    _L0_gnn_in = {k: v for k, v in _L0_gnn_all.items() if k in ('weight',)}
    del _L0_gnn_all

    def _L0_ffn_setup():
        import jax, jax.numpy as jnp
        import numpy as np
        B, S, D = (8, 512, 256)
        H = 4 * D
        CAPACITY = 0.5
        key = jax.random.key(seed)
        ks = jax.random.split(key, 6)
        x = jax.random.normal(ks[0], (B, S, D), dtype=jnp.float32)
        attention_mask = jnp.zeros((B, 1, 1, S), dtype=jnp.float32)
        wr = jax.random.normal(ks[1], (D, 1), dtype=jnp.float32) * 0.02
        br = jnp.zeros((1,), dtype=jnp.float32)
        w1 = jax.random.normal(ks[2], (D, H), dtype=jnp.float32) * 0.02
        b1 = jnp.zeros((H,), dtype=jnp.float32)
        w2 = jax.random.normal(ks[3], (H, D), dtype=jnp.float32) * 0.02
        b2 = jnp.zeros((D,), dtype=jnp.float32)
        return {'x': x, 'attention_mask': attention_mask, 'wr': wr, 'br': br, 'w1': w1, 'b1': b1, 'w2': w2, 'b2': b2}
    _L0_ffn_all = _L0_ffn_setup()
    _L0_ffn_in = {k: v for k, v in _L0_ffn_all.items() if k in ('attention_mask', 'wr', 'br', 'w1', 'b1', 'w2', 'b2')}
    del _L0_ffn_all

    def _L1_gnn_setup():
        import jax, jax.numpy as jnp
        import numpy as np
        N_NODES = 6250
        N_EDGES = 100000
        DIM = 256
        NEG_SLOPE = 0.01

        def _leaky_relu(x):
            return jnp.where(x >= 0, x, NEG_SLOPE * x)

        def _spmm(edge_row, edge_col, edge_val, x, n_nodes):
            msgs = edge_val[:, None] * x[edge_col]
            return jax.ops.segment_sum(msgs, edge_row, num_segments=n_nodes)
        key = jax.random.key(seed)
        ks = jax.random.split(key, 8)
        return {'ego_embeddings': jax.random.normal(ks[0], (N_NODES, DIM), dtype=jnp.float32), 'edge_row': jax.random.randint(ks[1], (N_EDGES,), 0, N_NODES, dtype=jnp.int32), 'edge_col': jax.random.randint(ks[2], (N_EDGES,), 0, N_NODES, dtype=jnp.int32), 'edge_val': jax.random.uniform(ks[3], (N_EDGES,), dtype=jnp.float32), 'W1': jax.random.normal(ks[4], (DIM, DIM), dtype=jnp.float32) * (1.0 / np.sqrt(DIM)), 'b1': jax.random.normal(ks[5], (DIM,), dtype=jnp.float32) * 0.01, 'W2': jax.random.normal(ks[6], (DIM, DIM), dtype=jnp.float32) * (1.0 / np.sqrt(DIM)), 'b2': jax.random.normal(ks[7], (DIM,), dtype=jnp.float32) * 0.01}
    _L1_gnn_all = _L1_gnn_setup()
    _L1_gnn_in = {k: v for k, v in _L1_gnn_all.items() if k in ('W1', 'b1', 'W2', 'b2')}
    del _L1_gnn_all

    def _L1_ffn_setup():
        import jax, jax.numpy as jnp
        import numpy as np
        D_MODEL = 256
        EXPERT_DIM = 512
        NUM_EXPERTS = 8
        TOP_K = 2
        SEQ_LEN = 256
        BATCH = 2
        key = jax.random.key(seed)
        ks = jax.random.split(key, 8)
        s = 0.02
        x = jax.random.normal(ks[0], (SEQ_LEN, BATCH, D_MODEL), dtype=jnp.float32)
        Wg = jax.random.normal(ks[1], (D_MODEL, NUM_EXPERTS), dtype=jnp.float32) * s
        bg = jax.random.normal(ks[2], (NUM_EXPERTS,), dtype=jnp.float32) * s
        bias = jnp.zeros((NUM_EXPERTS,), dtype=jnp.float32)
        W1 = jax.random.normal(ks[3], (NUM_EXPERTS, D_MODEL, EXPERT_DIM), dtype=jnp.float32) * s
        b1 = jax.random.normal(ks[4], (NUM_EXPERTS, EXPERT_DIM), dtype=jnp.float32) * s
        W2 = jax.random.normal(ks[5], (NUM_EXPERTS, EXPERT_DIM, D_MODEL), dtype=jnp.float32) * s
        b2 = jax.random.normal(ks[6], (NUM_EXPERTS, D_MODEL), dtype=jnp.float32) * s
        return {'x': x, 'Wg': Wg, 'bg': bg, 'bias': bias, 'W1': W1, 'b1': b1, 'W2': W2, 'b2': b2}
    _L1_ffn_all = _L1_ffn_setup()
    _L1_ffn_in = {k: v for k, v in _L1_ffn_all.items() if k in ('Wg', 'bg', 'bias', 'W1', 'b1', 'W2', 'b2')}
    del _L1_ffn_all
    return {'x': x, 'src': src, 'dst': dst, 'edge_type_16': edge_type_16, 'edge_weight': edge_weight, 'edge_weight1': edge_weight1, 'L0_gnn_weight': _L0_gnn_in['weight'], 'L0_ffn_attention_mask': _L0_ffn_in['attention_mask'], 'L0_ffn_wr': _L0_ffn_in['wr'], 'L0_ffn_br': _L0_ffn_in['br'], 'L0_ffn_w1': _L0_ffn_in['w1'], 'L0_ffn_b1': _L0_ffn_in['b1'], 'L0_ffn_w2': _L0_ffn_in['w2'], 'L0_ffn_b2': _L0_ffn_in['b2'], 'L1_gnn_W1': _L1_gnn_in['W1'], 'L1_gnn_b1': _L1_gnn_in['b1'], 'L1_gnn_W2': _L1_gnn_in['W2'], 'L1_gnn_b2': _L1_gnn_in['b2'], 'L1_ffn_Wg': _L1_ffn_in['Wg'], 'L1_ffn_bg': _L1_ffn_in['bg'], 'L1_ffn_bias': _L1_ffn_in['bias'], 'L1_ffn_W1': _L1_ffn_in['W1'], 'L1_ffn_b1': _L1_ffn_in['b1'], 'L1_ffn_W2': _L1_ffn_in['W2'], 'L1_ffn_b2': _L1_ffn_in['b2']}

def reference(x, src, dst, edge_type_16, edge_weight, edge_weight1, L0_gnn_weight, L0_ffn_attention_mask, L0_ffn_wr, L0_ffn_br, L0_ffn_w1, L0_ffn_b1, L0_ffn_w2, L0_ffn_b2, L1_gnn_W1, L1_gnn_b1, L1_gnn_W2, L1_gnn_b2, L1_ffn_Wg, L1_ffn_bg, L1_ffn_bias, L1_ffn_W1, L1_ffn_b1, L1_ffn_W2, L1_ffn_b2):
    import jax
    import jax.numpy as jnp

    def _L0_gnn_ref(h, weight, norm, src, dst, rel_type):
        import jax, jax.numpy as jnp
        import numpy as np
        N_NODES = 2500
        N_EDGES = 40000
        NUM_RELS = 16
        IN_FEAT = 256
        OUT_FEAT = 256
        transformed = jnp.einsum('ni,rio->rno', h, weight)
        msg = transformed[rel_type, src] * norm
        out = jax.ops.segment_sum(msg, dst, num_segments=h.shape[0])
        return out

    def _L0_ffn_ref(x, attention_mask, wr, br, w1, b1, w2, b2):
        import jax, jax.numpy as jnp
        import numpy as np
        B, S, D = (8, 512, 256)
        H = 4 * D
        CAPACITY = 0.5
        b, s, d = x.shape
        weights = (jnp.einsum('bsd,do->bso', x, wr) + br)[..., 0]
        k = max(1, int(CAPACITY * s))
        kk = k - 1 if k > 1 else 1
        _, idx = jax.lax.top_k(weights, k)
        sel_idx = idx[:, :kk]
        sel = jnp.take_along_axis(x, sel_idx[:, :, None], axis=1)
        h = jax.nn.gelu(jnp.einsum('bkd,dh->bkh', sel, w1) + b1)
        y = jnp.einsum('bkh,hd->bkd', h, w2) + b2
        w_sel = jnp.take_along_axis(weights, sel_idx, axis=1)
        y = y * w_sel[..., None]
        batch_idx = jnp.arange(b)[:, None]
        processed = jnp.zeros_like(x).at[batch_idx, sel_idx].set(y)
        return processed + x

    def _L1_gnn_ref(ego_embeddings, edge_row, edge_col, edge_val, W1, b1, W2, b2):
        import jax, jax.numpy as jnp
        import numpy as np
        N_NODES = 6250
        N_EDGES = 100000
        DIM = 256
        NEG_SLOPE = 0.01

        def _leaky_relu(x):
            return jnp.where(x >= 0, x, NEG_SLOPE * x)

        def _spmm(edge_row, edge_col, edge_val, x, n_nodes):
            msgs = edge_val[:, None] * x[edge_col]
            return jax.ops.segment_sum(msgs, edge_row, num_segments=n_nodes)
        side = _spmm(edge_row, edge_col, edge_val, ego_embeddings, ego_embeddings.shape[0])
        add_emb = ego_embeddings + side
        sum_emb = _leaky_relu(add_emb @ W1.T + b1)
        bi_emb = _leaky_relu(ego_embeddings * side @ W2.T + b2)
        return bi_emb + sum_emb

    def _L1_ffn_ref(x, Wg, bg, bias, W1, b1, W2, b2):
        import jax, jax.numpy as jnp
        import numpy as np
        D_MODEL = 256
        EXPERT_DIM = 512
        NUM_EXPERTS = 8
        TOP_K = 2
        SEQ_LEN = 256
        BATCH = 2
        x_flat = x.reshape(-1, D_MODEL)
        gate_logits = x_flat @ Wg + bg + bias
        topk_vals, topk_idx = jax.lax.top_k(gate_logits, TOP_K)
        topk_w = jax.nn.softmax(topk_vals, axis=-1)
        combine = (jax.nn.one_hot(topk_idx, NUM_EXPERTS, dtype=x.dtype) * topk_w[..., None]).sum(axis=1)
        h = jax.nn.relu(jnp.einsum('td,edh->teh', x_flat, W1) + b1)
        y = jnp.einsum('teh,ehd->ted', h, W2) + b2
        out = jnp.einsum('ted,te->td', y, combine)
        return out.reshape(x.shape)
    x = x + _L0_gnn_ref(_layernorm(x, axis=-1), L0_gnn_weight, edge_weight1, src, dst, edge_type_16)
    x = x + _L0_ffn_ref(_layernorm(x, axis=-1)[None], L0_ffn_attention_mask, L0_ffn_wr, L0_ffn_br, L0_ffn_w1, L0_ffn_b1, L0_ffn_w2, L0_ffn_b2)[0]
    x = x + _L1_gnn_ref(_layernorm(x, axis=-1), src, dst, edge_weight, L1_gnn_W1, L1_gnn_b1, L1_gnn_W2, L1_gnn_b2)
    x = x + _L1_ffn_ref(_layernorm(x, axis=-1)[None], L1_ffn_Wg, L1_ffn_bg, L1_ffn_bias, L1_ffn_W1, L1_ffn_b1, L1_ffn_W2, L1_ffn_b2)[0]
    return x

_drawn_inputs = setup_inputs


def setup_inputs(seed=0):
    import zlib

    import numpy as np

    out = dict(_drawn_inputs(seed))
    spreads = {'L0_ffn_b1': (0.0, 0.8), 'L0_ffn_b2': (0.0, 2.0), 'L1_ffn_bias': (0.0, 2.0)}
    factors = {'L0_ffn_wr': 8.0,
     'L0_ffn_w1': 8.0,
     'L0_ffn_w2': 8.0,
     'L1_gnn_b1': 200.0,
     'L1_gnn_b2': 200.0,
     'L1_ffn_Wg': 8.0,
     'L1_ffn_bg': 39.535,
     'L1_ffn_W1': 8.0,
     'L1_ffn_b1': 64.0,
     'L1_ffn_W2': 8.0,
     'L1_ffn_b2': 191.251}
    for name, (base, spread) in spreads.items():
        noise = np.random.default_rng([zlib.crc32(name.encode()), seed]).standard_normal(out[name].shape)
        drawn = base * np.exp(spread * noise) if base else spread * noise
        out[name] = jnp.asarray(drawn.astype(out[name].dtype))
    for name, factor in factors.items():
        out[name] = (out[name] * factor).astype(out[name].dtype)
    return out
```

```python
from contextlib import ExitStack

import concourse.bass as bass
from concourse import mybir

ALU = mybir.AluOpType
ACT = mybir.ActivationFunctionType
F32 = mybir.dt.float32
I32 = mybir.dt.int32
BF16 = mybir.dt.bfloat16
AX_X = mybir.AxisListType.X

P = 128
N = 6250
D = 256
E = 206250
RELS = 16
HIDDEN = 1024
EXPERTS, EHID = 8, 512
BLOCKS = -(-N // P)
NPAD = BLOCKS * P
KD = D // P
TG = 11
SLOTS = 3
STEP_EDGES = SLOTS * TG * P
STEPS = -(-E // STEP_EDGES)
GROUPS = STEPS * SLOTS
EPAD = STEPS * STEP_EDGES
WIN = 64
WINDOWS = NPAD // WIN
ACC_COLS = NPAD + WIN
CH = 512
T_CHUNKS = RELS * D // CH
PER_CHUNK = CH // D
HC = HIDDEN // P
EC = EHID // P
KEEP = max(1, N // 2) - 1
LANE_TILES = GROUPS * TG
PASS_TILES = SLOTS * TG
BATCH = CH // WINDOWS
SIZES = [BATCH, PASS_TILES % BATCH] + [BATCH] * (PASS_TILES // BATCH - 1)
SPLITS = [(sum(SIZES[:k]), n) for k, n in enumerate(SIZES)]
NSPLIT = len(SPLITS)
BG, BSLOTS = 8, 4
STEP_TILES = BG * BSLOTS
LAG = 4
BSTEPS = 54
BTILES = BSTEPS * STEP_TILES
REC = 3
MB = 7
BATCHES = BLOCKS // MB
EPS = 1e-5
BIG = 1e30
GATE_STEPS = 16
assert BTILES >= LANE_TILES + WINDOWS and BSTEPS == BLOCKS + LAG + 1
assert STEPS == BLOCKS and BLOCKS % 2 == 1 and BLOCKS % MB == 0


def gnn_kernel(nc, x, edge_ints, dst_lanes, src_lanes, norm0, norm1_lanes, wrel, wr, br, w1, b1, w2, b2,
               gw1t, gb1, gw2t, gb2, wg, bg, gbias, ew1, eb1, ew2, eb2, out):
    table0 = nc.dram_tensor("table0", (NPAD * RELS, D), F32, kind="Internal").ap()
    table1 = nc.dram_tensor("table1", (NPAD, D), F32, kind="Internal").ap()
    base_d = nc.dram_tensor("base_d", (NPAD, D), F32, kind="Internal").ap()
    x2_d = nc.dram_tensor("x2_d", (NPAD, D), F32, kind="Internal").ap()
    records = nc.dram_tensor("records", (BTILES * P, REC), I32, kind="Internal").ap()
    windows_d = nc.dram_tensor("windows_d", (1, BTILES), I32, kind="Internal").ap()
    table0_rows = table0.rearrange("(n r) d -> n (r d)", r=RELS)

    ctx = ExitStack()
    with ctx:
        def sb(name, shape, dt=F32):
            return ctx.enter_context(nc.sbuf_tensor(name, shape, dt))

        def pb(name):
            return ctx.enter_context(nc.psum_tensor(name, [P, CH], F32))

        def sem(name):
            return ctx.enter_context(nc.semaphore(name))

        acc = sb("acc", [P, KD, ACC_COLS])
        arena = sb("arena", [P, 2 * EXPERTS * KD * EHID])
        wrel_sb = arena[:, 0:RELS * KD * D].rearrange("p (k n) -> p k n", k=KD)
        tbuf = [arena[:, (2 + q) * RELS * D:(3 + q) * RELS * D] for q in range(2)]
        ew1_sb = arena[:, 0:EXPERTS * KD * EHID].rearrange("p (e k n) -> p e k n", e=EXPERTS, k=KD)
        ew2_sb = arena[:, EXPERTS * KD * EHID:].rearrange("p (e c n) -> p e c n", e=EXPERTS, c=EC)
        ring = sb("ring", [P, SLOTS, TG, D])
        ringf = ring[:, :, :, :].rearrange("p s t d -> p (s t d)")
        dst_all = ringf[:, 0:GROUPS * TG].bitcast(I32)
        bbuf = [ringf[:, q * MB * D:(q + 1) * MB * D].rearrange("p (m d) -> p m d", m=MB) for q in range(2)]
        hbuf = [ringf[:, (2 + q) * MB * D:(3 + q) * MB * D].rearrange("p (m d) -> p m d", m=MB) for q in range(2)]
        accf = acc[:, :, :].rearrange("p k n -> p (k n)")
        at = [0]

        def borrow(n, dt=F32):
            at[0] += n
            assert at[0] <= KD * ACC_COLS
            v = accf[:, at[0] - n:at[0]]
            return v if dt == F32 else v.bitcast(dt)

        zeros_rec = borrow(BTILES * REC)
        src_all = borrow(LANE_TILES, I32)
        rel_i = borrow(LANE_TILES, I32)
        wt_all = borrow(LANE_TILES)
        bkt = borrow(LANE_TILES // 2 + 1).bitcast(BF16)
        rel_bf = borrow(LANE_TILES // 2 + 1).bitcast(BF16)
        iota_b = sb("iota_b", [P, WINDOWS], BF16)
        ones_bf = sb("ones_bf", [P, P], BF16)
        before_bf = sb("before_bf", [P, P], BF16)
        carry = sb("carry", [P, WINDOWS])
        bcount = sb("bcount", [P, 4, WINDOWS])
        bcount_i = sb("bcount_i", [P, WINDOWS], I32)
        pos = sb("pos", [P, PASS_TILES])
        addr = sb("addr", [P, 4, PASS_TILES], I32)
        place_i = sb("place_i", [P, 2, PASS_TILES], I32)
        rec_out = sb("rec_out", [P, 2, PASS_TILES, REC], I32)
        bflag = sb("bflag", [P, 1], I32)
        onehot_all = sb("onehot", [P, SLOTS * TG * WIN])
        onehot = onehot_all[:, :].rearrange("p (s t w) -> p s t w", s=SLOTS, t=TG)
        bonehot = onehot_all[:, 0:STEP_TILES * WIN].rearrange("p (s t w) -> p s t w", s=BSLOTS, t=BG)
        inb = onehot_all[:, 0:PASS_TILES * WINDOWS // 2].bitcast(BF16).rearrange("p (t b) -> p t b", b=WINDOWS)
        bring = ringf[:, 0:STEP_TILES * D].rearrange("p (s t d) -> p s t d", s=BSLOTS, t=BG)
        rec_in = sb("rec_in", [P, BSLOTS, BG, REC], I32)
        eint = sb("eint", [P, SLOTS, 3, TG], I32)
        ewt = sb("ewt", [P, SLOTS, TG])
        idx = sb("idx", [P, SLOTS, TG], I32)
        drel = sb("drel", [P, SLOTS, TG])
        w1_sb = sb("w1_sb", [P, KD, HIDDEN])
        w2_sb = sb("w2_sb", [P, HC, D])
        b1_sb = sb("b1_sb", [P, HC])
        b2_sb = sb("b2_sb", [P, D])
        wr_sb = sb("wr_sb", [P, KD])
        br_sb = sb("br_sb", [P, 1])
        gw_sb = sb("gw_sb", [P, 2, KD, D])
        gb_sb = sb("gb_sb", [P, 2, D])
        wg_sb = sb("wg_sb", [P, KD, EXPERTS])
        gbias_sb = sb("gbias_sb", [P, 2, EXPERTS])
        gsum_sb = sb("gsum_sb", [P, EXPERTS])
        eb1_sb = sb("eb1_sb", [P, EXPERTS * EC])
        eb2_sb = sb("eb2_sb", [EXPERTS, D])
        ident = sb("ident", [P, P])
        ones = sb("ones", [P, P])
        before = sb("before", [P, P])
        iota_w = sb("iota_w", [P, WIN])
        wbase = sb("wbase", [P, WINDOWS])
        desc = sb("desc", [P, EXPERTS])
        eps_c = sb("eps_c", [P, 1])
        zero49 = sb("zero49", [P, BLOCKS])
        span = borrow(2 * GROUPS).rearrange("p (a g) -> p a g", a=2)
        spanr = borrow(2 * GROUPS).rearrange("p (a g) -> p a g", a=2)
        gmin = sb("gmin", [P, GROUPS])
        gmin_i = sb("gmin_i", [P, GROUPS], I32)
        gdiff = borrow(2 * GROUPS).rearrange("p (a g) -> p a g", a=2)
        earliest = sb("earliest", [P, GROUPS])
        worst = sb("worst", [P, 2])
        fits = sb("fits", [P, 2])
        flag = sb("flag", [P, 1], I32)
        xa = sb("xa", [P, 2, D])
        st6 = sb("st6", [P, MB, 6])
        mv = sb("mv", [P, MB, 2])
        std = sb("std", [P, MB])
        rstd = sb("rstd", [P, MB])
        h = sb("h", [P, D])
        xb = sb("xb", [P, D])
        hT = sb("hT", [P, 2, KD * P])
        accs = sb("accs", [P, KD * P])
        base = sb("base", [P, D])
        hid = sb("hid", [P, HC * P])
        y1 = sb("y1", [P, D])
        wcol = sb("wcol", [P, 1])
        wts = sb("wts", [P, BLOCKS])
        z = sb("z", [P, 2 * D])
        placed = z[:, 0:BATCH * WINDOWS].rearrange("p (t b) -> p t b", b=WINDOWS)
        window_made = ringf[0:1, 2048:2048 + BTILES].bitcast(I32)
        window_of = w1_sb[:, :, :].rearrange("p k n -> p (k n)")[0:1, 0:BTILES].bitcast(I32)
        hin, x3, addT, mulT = xa[:, 0, :], xa[:, 1, :], accs, base
        g8 = sb("g8", [P, 8, EXPERTS])
        gs = sb("gs", [P, 8])
        cTs = sb("cTs", [EXPERTS, P])
        ex = sb("ex", [P, 1])
        o = z[:, 0:D]
        key = y1[:, 0:4 * BLOCKS].bitcast(I32).rearrange("p (a b) -> p a b", a=4)
        kf = sb("kf", [P, 8, BLOCKS])
        sel = sb("sel", [P, BLOCKS])
        cnt = sb("cnt", [P, 1])
        srch = sb("srch", [P, 8])

        ps_seg = [pb(f"ps_seg{s}") for s in range(SLOTS)]
        ps_t = pb("ps_t")
        ps_m = ps_t
        ps_y2 = [pb("ps_y0"), pb("ps_y1")]
        ps_y = ps_y2[0]
        ps_h = [pb("ps_h0"), pb("ps_h1")]
        ps_count, ps_place, ps_tot = ps_y2[0], ps_h[1], ps_y2[1]
        t_banks = [ps_seg[0], ps_seg[1], ps_seg[2], ps_h[0]]

        s_w = sem("s_wrel_in")
        s_c = sem("s_consts_in")
        N_CONSTS = 16
        s_dst = sem("s_dst_in")
        s_ew = sem("s_expert_weights_in")
        s_k = sem("s_iotas")
        s_kv = sem("s_consts_made")
        s_span, s_spanr, s_win = sem("s_span"), sem("s_span_all"), sem("s_windows")
        s_ra = sem("s_acc_zero")
        a_x = [sem(f"a_x_in{q}") for q in range(2)]
        a_st, a_mv, a_std, a_rstd, a_h = (sem(f"a_{n}") for n in ("stats", "meanvar", "std", "rstd", "h"))
        a_tr, a_hT, a_ch = (sem(f"a_{n}") for n in ("transposed", "hT", "chunk"))
        a_ev_v, a_ev_s = sem("a_evicted_v"), sem("a_evicted_s")
        a_out = [sem(f"a_table_out{q}") for q in range(2)]
        seg = []
        for L in range(1):
            seg.append({
                "in": [sem(f"l{L}_edges_in{s}") for s in range(SLOTS)],
                "idx": [sem(f"l{L}_idx{s}") for s in range(SLOTS)],
                "rel": [sem(f"l{L}_rel{s}") for s in range(SLOTS)],
                "oh": [sem(f"l{L}_onehots{s}") for s in range(SLOTS)],
                "rows": [sem(f"l{L}_rows_in{s}") for s in range(SLOTS)],
                "mm": [sem(f"l{L}_window_summed{s}") for s in range(SLOTS)],
                "acc": [sem(f"l{L}_window_added{s}") for s in range(SLOTS)],
                "goh": sem(f"l{L}_all_onehots"), "gmm": sem(f"l{L}_all_summed"), "gacc": sem(f"l{L}_all_added"),
            })
        l0 = seg[0]
        c_rows, c_zero, c_zeroed = sem("c_rows_in"), sem("c_zeros_made"), sem("c_records_zeroed")
        c_pre, c_ob1, c_mm1 = sem("c_buckets"), sem("c_count_onehots"), sem("c_counted")
        c_end, c_cmp, c_win = sem("c_bucket_ends"), sem("c_tile_compared"), sem("c_tile_windows")
        c_wout, c_wback = sem("c_windows_out"), sem("c_windows_back")
        c_bflag = sem("c_bflag")
        c_ob, c_mm, c_take = sem("c_onehots"), sem("c_ranked"), sem("c_placed")
        c_addr, c_rec = sem("c_addresses"), sem("c_records")
        c_out = [sem(f"c_scattered{q}") for q in range(2)]
        b_in, b_oh, b_rows = ([sem(f"b_{n}{s}") for s in range(BSLOTS)] for n in ("records", "onehots", "rows"))
        b_mm, b_add = sem("b_summed"), sem("b_added")
        d0 = {n: sem(f"d0_{n}") for n in
              ("accs", "trA", "x_in", "x1", "bs", "mv", "std", "rstd", "h", "base", "out", "trH", "hT", "rt",
               "w", "wts", "hid", "gelu", "y", "y1", "yw")}
        q_v, q_mm = sem("select_step"), sem("select_counted")
        m_in = [sem(f"m_base_in{q}") for q in range(2)]
        m_out = [sem(f"m_out{q}") for q in range(2)]
        m_x2, m_bs, m_mv, m_std, m_rstd, m_h = (sem(f"m_{n}") for n in ("x2", "bs", "mv", "std", "rstd", "h"))
        d1 = {n: sem(f"d1_{n}") for n in
              ("h_in", "x_in", "tr1", "add", "mul", "g", "z", "zl", "zs", "x3", "bs", "mv", "std", "rstd", "h",
               "trH", "hT", "lg", "gate", "exp", "ct", "cts", "b2", "o0", "hid", "relu", "y", "o", "out")}

        block = ctx.enter_context(nc.Block())

        def wait(eng, signal, value):
            if not isinstance(value, int) or value > 0:
                eng.wait_ge(signal, value)

        def hold(eng):
            eng.nop(nofuse=True)

        def both_ways0(eng, early, group_work, window_work, block_work):
            with eng.If(early):
                group_work(0)
                group_work(1)
                block_work(0)
                with eng.Fori(2, STEPS) as i:
                    group_work(i)
                    block_work(i - 1)
                block_work(BLOCKS - 1)
            with eng.Else():
                window_work()
                block_work(0)
                with eng.Fori(1, BLOCKS) as b:
                    block_work(b)

        def both_ways1(eng, early, group_work, block_work):
            group_work(0)
            with eng.If(early):
                with eng.Fori(1, LAG) as i:
                    group_work(i)
                group_work(LAG)
                block_work(0)
                with eng.Fori(LAG + 1, LAG + BLOCKS) as i:
                    group_work(i)
                    block_work(i - LAG)
                group_work(BSTEPS - 1)
            with eng.Else():
                with eng.Fori(1, BSTEPS) as i:
                    group_work(i)
                block_work(0)
                with eng.Fori(1, BLOCKS) as b:
                    block_work(b)

        def early_flag0(eng):
            eng.wait_ge(s_win, 1)
            return eng.value_load(flag[0:1, 0:1], min_val=0, max_val=1)

        def early_flag1(eng):
            eng.wait_ge(c_bflag, 1)
            return eng.value_load(bflag[0:1, 0:1], min_val=0, max_val=1)

        @block.sync
        def _(sp):
            def load_x(b, q):
                wait(sp, a_h, b - 1)
                sp.dma_start(xa[:, q, :], x[bass.ds(b * P, P), :]).then_inc(a_x[q], 16)

            sp.dma_start(src_all, src_lanes).then_inc(c_rows, 16)
            sp.dma_start(dst_all, dst_lanes).then_inc(s_dst, 16)
            sp.dma_start(wt_all, norm1_lanes).then_inc(c_rows, 16)
            load_x(0, 0)
            load_x(1, 1)
            for k in range(KD):
                sp.dma_start(wrel_sb[:, k, :], wrel[k].rearrange("p r o -> p (r o)")).then_inc(s_w, 16)
            sp.wait_ge(c_zero, 1)
            sp.dma_start(records.rearrange("(p n) r -> p (n r)", p=P), zeros_rec.bitcast(I32)).then_inc(c_zeroed, 16)
            for dst, src in (
                (w1_sb[:, :, :], w1.rearrange("(k p) n -> p k n", p=P)),
                (w2_sb[:, :, :], w2.rearrange("(c p) n -> p c n", p=P)),
                (b1_sb[:, :], b1), (b2_sb[:, :], b2.partition_broadcast(P)),
                (wr_sb[:, :], wr), (br_sb[:, :], br.partition_broadcast(P)),
                (gw_sb[:, 0, :, :], gw1t.rearrange("(k p) n -> p k n", p=P)),
                (gw_sb[:, 1, :, :], gw2t.rearrange("(k p) n -> p k n", p=P)),
                (gb_sb[:, 0, :], gb1.partition_broadcast(P)), (gb_sb[:, 1, :], gb2.partition_broadcast(P)),
                (wg_sb[:, 0, :], wg[0:P, :]), (wg_sb[:, 1, :], wg[P:D, :]),
                (gbias_sb[:, 0, :], bg.partition_broadcast(P)), (gbias_sb[:, 1, :], gbias.partition_broadcast(P)),
                (eb1_sb[:, :], eb1), (eb2_sb[:, :], eb2),
            ):
                sp.dma_start(dst, src).then_inc(s_c, 16)
            sp.wait_ge(c_win, 4)
            sp.dma_start(windows_d, window_made).then_inc(c_wout, 16)
            load_x(2, 0)
            with sp.Fori(1, BLOCKS // 2) as j:
                load_x(2 * j + 1, 1)
                load_x(2 * j + 2, 0)

            sp.wait_ge(a_ch, T_CHUNKS * BLOCKS)
            sp.wait_ge(a_out[0], 16 * (BLOCKS // 2 + 1))
            sp.wait_ge(a_out[1], 16 * (BLOCKS // 2))
            sp.dma_start(ew1_sb, ew1.rearrange("e (k p) n -> p e k n", p=P)).then_inc(s_ew, 16)
            sp.dma_start(ew2_sb, ew2.rearrange("e (c p) n -> p e c n", p=P)).then_inc(s_ew, 16)

            def load_edges(g, s):
                sp.dma_start(eint[:, s, :, :], edge_ints[bass.ds(g, 1), :, :]
                             .rearrange("g p n -> (g p) n")).then_inc(l0["in"][s], 16)
                sp.dma_start(ewt[:, s, :], norm0[bass.ds(g, 1), :, :]
                             .rearrange("g p n -> (g p) n")).then_inc(l0["in"][s], 16)

            def load_step(i):
                for s in range(SLOTS):
                    wait(sp, l0["oh"][s], i)
                    load_edges(SLOTS * i + s, s)

            def all_windows():
                load_edges(0, 0)
                with sp.Fori(1, GROUPS) as g:
                    sp.wait_ge(l0["gacc"], g * WINDOWS + 1)
                    load_edges(g, 0)

            def block0(b):
                wait(sp, d0["x1"], b)
                sp.dma_start(xb[:, :], x[bass.ds(b * P, P), :]).then_inc(d0["x_in"], 16)

            def block1(b):
                wait(sp, d1["tr1"], b)
                sp.dma_start(hin, table1[bass.ds(b * P, P), :]).then_inc(d1["h_in"], 16)
                wait(sp, d1["x3"], b)
                sp.dma_start(xb[:, :], x2_d[bass.ds(b * P, P), :]).then_inc(d1["x_in"], 16)

            with sp.If(early_flag0(sp)):
                load_step(0)
                load_step(1)
                block0(0)
                with sp.Fori(2, STEPS) as i:
                    load_step(i)
                    block0(i - 1)
                block0(BLOCKS - 1)
            with sp.Else():
                all_windows()
                block0(0)
                with sp.Fori(1, BLOCKS) as b:
                    block0(b)

            sp.wait_ge(d0["hid"], 2 * BLOCKS)
            sp.wait_ge(c_wout, 16)
            sp.dma_start(window_of, windows_d).then_inc(c_wback, 16)

            sp.wait_ge(d0["out"], 16 * BLOCKS)

            def rows(dram, t):
                return dram[bass.ds(t * MB * P, MB * P), :].rearrange("(m p) d -> p m d", p=P)

            for t in range(BATCHES + 1):
                if t < BATCHES:
                    if t >= 2:
                        sp.wait_ge(m_out[t % 2], 32 * (t // 2))
                    sp.dma_start(bbuf[t % 2], rows(base_d, t)).then_inc(m_in[t % 2], 16)
                if t >= 1:
                    sp.wait_ge(m_x2, MB * t)
                    sp.dma_start(rows(x2_d, t - 1), bbuf[(t - 1) % 2]).then_inc(m_out[(t - 1) % 2], 16)
                    sp.wait_ge(m_h, MB * t)
                    sp.dma_start(rows(table1, t - 1), hbuf[(t - 1) % 2]).then_inc(m_out[(t - 1) % 2], 16)

            def load_records(i, s):
                wait(sp, b_rows[s], 16 * BG * i)
                wait(sp, b_oh[s], i)
                sp.dma_start(rec_in[:, s, :, :].rearrange("p t r -> p (t r)"),
                             records[bass.ds((BSLOTS * i + s) * BG * P, BG * P), :]
                             .rearrange("(p t) r -> p (t r)", p=P)).then_inc(b_in[s], 16)

            def load_record_step(i):
                for s in range(BSLOTS):
                    load_records(i, s)

            sp.wait_ge(c_out[0], 16 * PASS_TILES * (BLOCKS // 2 + 1))
            sp.wait_ge(c_out[1], 16 * PASS_TILES * (BLOCKS // 2))
            load_record_step(0)
            sp.wait_ge(m_out[0], 32 * ((BATCHES + 1) // 2))
            sp.wait_ge(m_out[1], 32 * (BATCHES // 2))
            with sp.If(early_flag1(sp)):
                with sp.Fori(1, LAG + 2) as i:
                    load_record_step(i)
                block1(0)
                with sp.Fori(LAG + 1, LAG + BLOCKS) as i:
                    load_record_step(i + 1)
                    block1(i - LAG)
            with sp.Else():
                with sp.Fori(1, BSTEPS) as i:
                    load_record_step(i)
                block1(0)
                with sp.Fori(1, BLOCKS) as b:
                    block1(b)
            sp.wait_ge(d1["out"], 16 * BLOCKS)

        @block.gpsimd
        def _(pool):
            pool.iota(iota_w[:, :], [[1, WIN]], base=0, channel_multiplier=0,
                      allow_small_or_imprecise_dtypes=True).then_inc(s_k, 1)
            pool.iota(wbase[:, :], [[WIN, WINDOWS]], base=0, channel_multiplier=0,
                      allow_small_or_imprecise_dtypes=True).then_inc(s_k, 1)
            pool.iota(desc[:, :], [[-1, EXPERTS]], base=EXPERTS, channel_multiplier=0,
                      allow_small_or_imprecise_dtypes=True).then_inc(s_k, 1)
            pool.iota(earliest[:, :], [[P, STEPS], [0, SLOTS]], base=-P, channel_multiplier=0,
                      allow_small_or_imprecise_dtypes=True).then_inc(s_k, 1)
            pool.iota(kf[:, 7, :], [[P, BLOCKS]], base=0, channel_multiplier=1,
                      allow_small_or_imprecise_dtypes=True).then_inc(s_k, 1)
            pool.iota(bcount[:, 0, :], [[1, WINDOWS]], base=0, channel_multiplier=0,
                      allow_small_or_imprecise_dtypes=True).then_inc(s_k, 1)
            pool.iota(z[:, 0:BTILES // 4], [[1, BTILES // 4]], base=0, channel_multiplier=0,
                      allow_small_or_imprecise_dtypes=True).then_inc(s_k, 1)
            pool.iota(kf[:, 6, :], [[STEP_TILES, BLOCKS]], base=STEP_TILES * (LAG + 1), channel_multiplier=0,
                      allow_small_or_imprecise_dtypes=True).then_inc(s_k, 1)
            pool.memset(ident[:, :], 0.0).then_inc(s_k, 1)
            pool.memset(before[:, :], 0.0).then_inc(s_k, 1)
            pool.wait_ge(s_k, 10)
            pool.affine_select(out=ident[:, :], in_=ident[:, :], compare_op=ALU.not_equal, fill=1.0, base=0,
                               pattern=[[-1, P]], channel_multiplier=1).then_inc(s_k, 1)
            pool.affine_select(out=before[:, :], in_=before[:, :], compare_op=ALU.is_ge, fill=1.0, base=0,
                               pattern=[[-1, P]], channel_multiplier=1).then_inc(s_k, 1)
            pool.wait_ge(s_span, 3)
            pool.partition_all_reduce(spanr[:, :, :].rearrange("p a g -> p (a g)"),
                                      span[:, :, :].rearrange("p a g -> p (a g)"), P,
                                      bass.bass_isa.ReduceOp.max).then_inc(s_spanr, 1)
            def scatter(i, q):
                wait(pool, c_rec, 4 * (i + 1))
                hold(pool)
                for t in range(PASS_TILES):
                    pool.indirect_dma_start(records, bass.IndirectOffsetOnAxis(ap=place_i[:, q, t:t + 1], axis=0),
                                            rec_out[:, q, t, :], None).then_inc(c_out[q], 16)

            pool.wait_ge(c_zeroed, 16)
            scatter(0, 0)
            with pool.Fori(0, BLOCKS // 2) as j:
                scatter(2 * j + 1, 1)
                scatter(2 * j + 2, 0)

            def gather(s):
                for t in range(TG):
                    pool.indirect_dma_start(ring[:, s, t, :], None, table0,
                                            bass.IndirectOffsetOnAxis(ap=idx[:, s, t:t + 1], axis=0)
                                            ).then_inc(l0["rows"][s], 16)

            def group(i):
                for s in range(SLOTS):
                    wait(pool, l0["idx"][s], i + 1)
                    wait(pool, l0["mm"][s], i)
                    hold(pool)
                    gather(s)

            def all_windows():
                with pool.Fori(0, GROUPS) as g:
                    pool.wait_ge(l0["idx"][0], g + 1)
                    pool.wait_ge(l0["gmm"], g * WINDOWS + 1)
                    hold(pool)
                    gather(0)

            pool.wait_ge(c_wout, 16)
            pool.wait_ge(a_out[0], 16 * (BLOCKS // 2 + 1))
            pool.wait_ge(a_out[1], 16 * (BLOCKS // 2))
            with pool.If(early_flag0(pool)):
                group(0)
                with pool.Fori(1, STEPS) as i:
                    group(i)
            with pool.Else():
                all_windows()

            def record_group(i):
                for s in range(BSLOTS):
                    wait(pool, b_in[s], 16 * (i + 1))
                    if not isinstance(i, int):
                        pool.wait_ge(b_mm, 2 * BSLOTS * (i - 1) + 2 * s + 2)
                    hold(pool)
                    for t in range(BG):
                        pool.indirect_dma_start(bring[:, s, t, :], None, table1,
                                                bass.IndirectOffsetOnAxis(ap=rec_in[:, s, t, 0:1], axis=0)
                                                ).then_inc(b_rows[s], 16)

            pool.wait_ge(m_out[0], 32 * ((BATCHES + 1) // 2))
            pool.wait_ge(m_out[1], 32 * (BATCHES // 2))
            record_group(0)
            with pool.Fori(1, BSTEPS) as i:
                record_group(i)

        @block.vector
        def _(dve):
            dve.memset(ones[:, :], 1.0).then_inc(s_kv, 1)
            dve.memset(eps_c[:, :], EPS).then_inc(s_kv, 1)
            dve.memset(zero49[:, :], 0.0).then_inc(s_kv, 1)
            dve.memset(zeros_rec, 0.0).then_inc(c_zero, 1)
            dve.memset(cnt[:, :], 0.0).then_inc(a_ev_v, 2)
            dve.memset(srch[:, :], 0.0).then_inc(a_ev_s, 2)
            dve.memset(ones_bf[:, :], 1.0).then_inc(s_kv, 1)
            dve.wait_ge(s_k, 12)
            dve.tensor_copy(before_bf[:, :], before[:, :]).then_inc(s_kv, 1)
            dve.tensor_copy(iota_b[:, :], bcount[:, 0, :]).then_inc(s_kv, 1)

            dve.wait_ge(c_rows, 32)
            dve.tensor_scalar(rel_i, src_all, WIN - 1, None, ALU.bitwise_and).then_inc(c_pre, 1)
            dve.wait_ge(c_pre, 1)
            dve.tensor_copy(rel_bf[:, 0:LANE_TILES], rel_i).then_inc(c_pre, 1)
            dve.wait_ge(c_pre, 2)
            dve.tensor_scalar(rel_i, src_all, WIN.bit_length() - 1, None, ALU.logical_shift_right).then_inc(c_pre, 1)
            dve.wait_ge(c_pre, 3)
            dve.tensor_copy(bkt[:, 0:LANE_TILES], rel_i).then_inc(c_pre, 1)
            dve.wait_ge(c_pre, 4)
            dve.wait_ge(s_kv, 6)

            def bucket_onehots(i, k, done):
                t0, n = SPLITS[k]
                dve.tensor_tensor(inb[:, t0:t0 + n, :], iota_b[:, :].unsqueeze(1).broadcast_to([P, n, WINDOWS]),
                                  bkt[:, bass.ds(PASS_TILES * i + t0, n)].unsqueeze(2).broadcast_to([P, n, WINDOWS]),
                                  ALU.is_equal).then_inc(done, 1)

            def count_pass(i):
                for k in range(NSPLIT):
                    if not isinstance(i, int):
                        dve.wait_ge(c_mm1, NSPLIT * (i - 1) + k + 1)
                    bucket_onehots(i, k, c_ob1)

            count_pass(0)
            with dve.Fori(1, BLOCKS) as i:
                count_pass(i)

            ends = [0]

            def link(ins):
                ends[0] += 1
                ins.then_inc(c_end, 1)
                dve.wait_ge(c_end, ends[0])

            dve.wait_ge(c_mm1, NSPLIT * BLOCKS)
            link(dve.tensor_reduce(bcount[:, 0, :], ps_count[:, 0:BATCH * WINDOWS]
                                   .rearrange("p (t b) -> p b t", b=WINDOWS), AX_X, ALU.add))
            link(dve.tensor_scalar(bcount[:, 0, :], bcount[:, 0, :], float(P - 1), None, ALU.add))
            link(dve.tensor_copy(bcount_i[:, :], bcount[:, 0, :]))
            link(dve.tensor_scalar(bcount_i[:, :], bcount_i[:, :], 7, None, ALU.logical_shift_right))
            link(dve.tensor_copy(bcount[:, 1, :], bcount_i[:, :]))
            link(dve.memset(bcount[:, 0, :], 0.0))
            link(dve.tensor_tensor_scan(bcount[:, 2, :], bcount[:, 1, :], bcount[:, 0, :], 0.0, ALU.add, ALU.add))
            link(dve.tensor_tensor(carry[:, :], bcount[:, 2, :], bcount[:, 1, :], ALU.subtract))
            link(dve.tensor_scalar(carry[:, :], carry[:, :], float(P), None, ALU.mult))
            link(dve.tensor_tensor(bcount[:, 3, :], bcount[:, 2, :], ident[:, 0:WINDOWS], ALU.mult))
            link(dve.tensor_reduce(cnt[:, :], bcount[:, 3, :], AX_X, ALU.add))
            quarter = BTILES // 4
            passed = inb[:, :, :].rearrange("p t b -> p (t b)")
            for r in range(4):
                wait(dve, c_win, r)
                dve.tensor_scalar(passed[0:WINDOWS, 0:quarter], z[0:WINDOWS, 0:quarter], float(r * quarter),
                                  cnt[0:WINDOWS, 0:1], ALU.add, ALU.is_ge).then_inc(c_cmp, 1)
                dve.wait_ge(c_mm1, NSPLIT * BLOCKS + r + 1)
                dve.tensor_scalar(window_made[0:1, r * quarter:(r + 1) * quarter], ps_count[0:1, 0:quarter],
                                  float(WINDOWS - 1), float(WIN), ALU.min, ALU.mult).then_inc(c_win, 1)
            ends_of_blocks = bcount[:, 2, :].rearrange("p (b two) -> p b two", two=2)[:, :, 1]
            link(dve.tensor_tensor(kf[:, 5, :], ends_of_blocks, kf[:, 6, :], ALU.subtract))
            link(dve.tensor_reduce(srch[:, 0:1], kf[:, 5, :], AX_X, ALU.max))
            dve.tensor_scalar(bflag[:, :], srch[:, 0:1], 0.0, None, ALU.is_le).then_inc(c_bflag, 1)

            dve.wait_ge(s_dst, 16)
            dstg = dst_all.rearrange("p (g t) -> p g t", t=TG)
            dve.tensor_reduce(gmin[:, :], dstg, AX_X, ALU.min).then_inc(s_span, 1)
            dve.tensor_reduce(span[:, 1, :], dstg, AX_X, ALU.max).then_inc(s_span, 1)
            dve.wait_ge(s_span, 1)
            dve.tensor_scalar(span[:, 0, :], gmin[:, :], -1.0, None, ALU.mult).then_inc(s_span, 1)
            dve.wait_ge(s_spanr, 1)
            dve.wait_ge(s_k, 12)
            dve.tensor_scalar(gmin[:, :], spanr[:, 0, :], -1.0, None, ALU.mult).then_inc(s_span, 1)
            dve.wait_ge(s_span, 4)
            dve.tensor_copy(gmin_i[:, :], gmin[:, :]).then_inc(s_span, 1)
            dve.tensor_tensor(gdiff[:, 0, :], spanr[:, 1, :], gmin[:, :], ALU.subtract).then_inc(s_span, 1)
            dve.tensor_tensor(gdiff[:, 1, :], earliest[:, :], gmin[:, :], ALU.subtract).then_inc(s_span, 1)
            dve.wait_ge(s_span, 7)
            dve.tensor_reduce(worst[:, :], gdiff[:, :, :], AX_X, ALU.max).then_inc(s_span, 1)
            dve.wait_ge(s_span, 8)
            dve.tensor_scalar(fits[:, 0:1], worst[:, 0:1], float(WIN - 1), None, ALU.is_le).then_inc(s_span, 1)
            dve.tensor_scalar(fits[:, 1:2], worst[:, 1:2], 0.0, None, ALU.is_le).then_inc(s_span, 1)
            dve.wait_ge(s_span, 10)
            dve.tensor_tensor(flag[:, :], fits[:, 0:1], fits[:, 1:2], ALU.mult).then_inc(s_win, 1)

            def norm_block(b, q, times):
                dve.wait_ge(a_x[q], 16 * times + 16)
                dve.bn_stats(st6[:, 0, :], xa[:, q, :]).then_inc(a_st, 1)
                dve.wait_ge(a_st, b + 1)
                hold(dve)
                dve.bn_aggr(mv[:, 0, :], st6[:, 0, :]).then_inc(a_mv, 1)
                dve.wait_ge(a_std, b + 1)
                dve.reciprocal(rstd[:, 0:1], std[:, 0:1]).then_inc(a_rstd, 1)
                dve.wait_ge(a_rstd, b + 1)
                wait(dve, a_tr, b)
                dve.tensor_scalar(h[:, :], xa[:, q, :], mv[:, 0, 0:1], rstd[:, 0:1],
                                  ALU.subtract, ALU.mult).then_inc(a_h, 1)

            def evict(b, q, times, c):
                dve.wait_ge(a_ch, T_CHUNKS * b + c + 1)
                if c == 0:
                    wait(dve, a_out[q], 16 * times)
                dve.tensor_copy(tbuf[q][:, c * CH:(c + 1) * CH], t_banks[c % 4][:, :]).then_inc(a_ev_v, 1)

            ADDR_STEPS = NSPLIT + 6

            def place_split(i, k):
                t0, n = SPLITS[k]
                m = NSPLIT * i + k
                dve.wait_ge(c_mm, m + 1)
                wait(dve, c_addr, ADDR_STEPS * i + k)
                dve.tensor_tensor(placed[:, 0:n, :], ps_place[:, 0:n * WINDOWS]
                                  .rearrange("p (t b) -> p t b", b=WINDOWS),
                                  carry[:, :].unsqueeze(1).broadcast_to([P, n, WINDOWS]),
                                  ALU.add).then_inc(c_take, 1)
                dve.wait_ge(c_take, 3 * m + 1)
                dve.tensor_tensor(placed[:, 0:n, :], placed[:, 0:n, :], inb[:, t0:t0 + n, :],
                                  ALU.mult).then_inc(c_take, 1)
                dve.tensor_tensor(carry[:, :], carry[:, :], ps_tot[:, 0:WINDOWS], ALU.add).then_inc(c_take, 1)
                dve.wait_ge(c_take, 3 * m + 3)
                dve.tensor_reduce(pos[:, t0:t0 + n], placed[:, 0:n, :], AX_X, ALU.add).then_inc(c_addr, 1)

            def finish_pass(i, q, times):
                n = [NSPLIT]

                def link(ins):
                    n[0] += 1
                    ins.then_inc(c_addr, 1)
                    dve.wait_ge(c_addr, ADDR_STEPS * i + n[0])

                dve.wait_ge(c_addr, ADDR_STEPS * i + NSPLIT)
                link(dve.tensor_copy(addr[:, 0, :], pos[:, :]))
                link(dve.tensor_scalar(addr[:, 1, :], addr[:, 0, :], -BG * P, None, ALU.bitwise_and))
                link(dve.tensor_scalar(addr[:, 2, :], addr[:, 0, :], P - 1, BG.bit_length() - 1,
                                       ALU.bitwise_and, ALU.logical_shift_left))
                link(dve.tensor_scalar(addr[:, 3, :], addr[:, 0, :], P.bit_length() - 1, BG - 1,
                                       ALU.logical_shift_right, ALU.bitwise_and))
                link(dve.tensor_tensor(addr[:, 1, :], addr[:, 1, :], addr[:, 2, :], ALU.bitwise_or))
                wait(dve, c_out[q], 16 * PASS_TILES * times)
                link(dve.tensor_copy(addr[:, 2, :], addr[:, 3, :]))
                assert n[0] == ADDR_STEPS
                dve.tensor_tensor(place_i[:, q, :], addr[:, 1, :], addr[:, 3, :],
                                  ALU.bitwise_or).then_inc(c_rec, 1)
                tiles = bass.ds(PASS_TILES * i, PASS_TILES)
                dve.tensor_copy(rec_out[:, q, :, 0], dst_all[:, tiles]).then_inc(c_rec, 1)
                dve.tensor_copy(rec_out[:, q, :, 1].bitcast(F32), rel_bf[:, tiles]).then_inc(c_rec, 1)
                dve.tensor_copy(rec_out[:, q, :, 2].bitcast(F32), wt_all[:, tiles]).then_inc(c_rec, 1)

            def table_and_places(b, q, times):
                bucket_onehots(b, 0, c_ob)
                for c in range(T_CHUNKS):
                    if c + 1 < NSPLIT:
                        bucket_onehots(b, c + 1, c_ob)
                    if c % 2 == 0:
                        evict(b, q, times, c)
                    if c < NSPLIT:
                        place_split(b, c)
                finish_pass(b, q, times)

            norm_block(0, 0, 0)
            norm_block(1, 1, 0)
            table_and_places(0, 0, 0)
            norm_block(2, 0, 1)
            table_and_places(1, 1, 0)
            with dve.Fori(1, BLOCKS // 2) as j:
                norm_block(2 * j + 1, 1, j)
                table_and_places(2 * j, 0, j)
                norm_block(2 * j + 2, 0, j + 1)
                table_and_places(2 * j + 1, 1, j)
            table_and_places(BLOCKS - 1, 0, BLOCKS // 2)
            dve.wait_ge(s_c, 16 * N_CONSTS)
            dve.tensor_tensor(gsum_sb[:, :], gbias_sb[:, 0, :], gbias_sb[:, 1, :], ALU.add).then_inc(s_kv, 1)
            dve.wait_ge(c_zeroed, 16)
            dve.wait_ge(c_rec, 4 * BLOCKS)
            dve.memset(acc[:, :, :], 0.0).then_inc(s_ra, 1)
            dve.wait_ge(s_ra, 1)

            def make_idx(s):
                dve.scalar_tensor_tensor(out=idx[:, s, :], in0=eint[:, s, 0, :], scalar=float(RELS),
                                         in1=eint[:, s, 1, :], op0=ALU.mult,
                                         op1=ALU.add).then_inc(l0["idx"][s], 1)

            def prepare(i, s):
                wait(dve, l0["in"][s], 32 * (i + 1))
                wait(dve, l0["rows"][s], 16 * TG * i)
                make_idx(s)
                dve.tensor_scalar(drel[:, s, :], eint[:, s, 2, :], gmin[:, bass.ds(SLOTS * i + s, 1)], None,
                                  ALU.subtract).then_inc(l0["rel"][s], 1)
                wait(dve, l0["rel"][s], i + 1)
                wait(dve, l0["mm"][s], i)
                for t in range(TG):
                    ins = dve.tensor_scalar(onehot[:, s, t, :], iota_w[:, :], drel[:, s, t:t + 1],
                                            ewt[:, s, t:t + 1], ALU.is_equal, ALU.mult)
                ins.then_inc(l0["oh"][s], 1)

            def add_window(i, s):
                at = dve.value_load(gmin_i[0:1, bass.ds(SLOTS * i + s, 1)], min_val=0, max_val=N - 1)
                wait(dve, l0["mm"][s], i + 1)
                wait(dve, l0["acc"][(s - 1) % SLOTS], i + (s > 0))
                cols = acc[:, :, bass.ds(at, WIN)]
                dve.tensor_tensor(cols, cols, ps_seg[s][:, 0:KD * WIN].rearrange("p (k w) -> p k w", k=KD),
                                  ALU.add).then_inc(l0["acc"][s], 1)

            def group(i):
                for s in range(SLOTS):
                    add_window(i, s)
                    prepare(i + 1, s)

            def all_windows():
                dve.memset(cnt[:, :], 0.0).then_inc(l0["gmm"], 1)
                dve.memset(srch[:, :], 0.0).then_inc(l0["gacc"], 1)
                with dve.Fori(0, GROUPS) as g:
                    dve.wait_ge(l0["in"][0], 32 * (g + 1))
                    dve.wait_ge(l0["gmm"], g * WINDOWS + 1)
                    make_idx(0)
                    with dve.Fori(0, WINDOWS) as w:
                        k = g * WINDOWS + w
                        dve.wait_ge(l0["gmm"], k + 1)
                        dve.tensor_scalar(drel[:, 0, :], eint[:, 0, 2, :], wbase[:, bass.ds(w, 1)], None,
                                          ALU.subtract).then_inc(l0["rel"][0], 1)
                        dve.wait_ge(l0["rel"][0], k + 1)
                        for t in range(TG):
                            ins = dve.tensor_scalar(onehot[:, 0, t, :], iota_w[:, :], drel[:, 0, t:t + 1],
                                                    ewt[:, 0, t:t + 1], ALU.is_equal, ALU.mult)
                        ins.then_inc(l0["goh"], 1)
                        dve.wait_ge(l0["gmm"], k + 2)
                        dve.wait_ge(l0["gacc"], k + 1)
                        cols = acc[:, :, bass.ds(w * WIN, WIN)]
                        dve.tensor_tensor(cols, cols,
                                          ps_seg[0][:, 0:KD * WIN].rearrange("p (k w) -> p k w", k=KD),
                                          ALU.add).then_inc(l0["gacc"], 1)
                dve.wait_ge(l0["gacc"], GROUPS * WINDOWS + 1)

            def block_norm(v, b, src, scratch_h):
                dve.bn_stats(st6[:, 0, :], src).then_inc(v["bs"], 1)
                dve.wait_ge(v["bs"], b + 1)
                hold(dve)
                dve.bn_aggr(mv[:, 0, :], st6[:, 0, :]).then_inc(v["mv"], 1)
                dve.wait_ge(v["std"], b + 1)
                dve.reciprocal(rstd[:, 0:1], std[:, 0:1]).then_inc(v["rstd"], 1)
                dve.wait_ge(v["rstd"], b + 1)
                wait(dve, v["trH"], b)
                dve.tensor_scalar(scratch_h, src, mv[:, 0, 0:1], rstd[:, 0:1],
                                  ALU.subtract, ALU.mult).then_inc(v["h"], 1)

            def block0(b):
                blk = acc[:, :, bass.ds(b * P, P)]
                wait(dve, d0["trA"], b)
                dve.tensor_copy(accs[:, :].rearrange("p (k c) -> p k c", k=KD), blk).then_inc(d0["accs"], 1)
                dve.wait_ge(d0["trA"], b + 1)
                dve.wait_ge(d0["x_in"], 16 * (b + 1))
                wait(dve, d0["base"], b)
                dve.tensor_tensor(z[:, 0:D], ps_t[:, 0:D], xb[:, :], ALU.add).then_inc(d0["x1"], 1)
                dve.wait_ge(d0["x1"], b + 1)
                block_norm(d0, b, z[:, 0:D], h[:, :])
                dve.wait_ge(d0["h"], b + 1)
                wait(dve, d0["out"], 16 * b)
                dve.tensor_tensor(base[:, :], z[:, 0:D], h[:, :], ALU.add).then_inc(d0["base"], 1)
                dve.wait_ge(d0["rt"], b + 1)
                wait(dve, d0["yw"], b)
                dve.tensor_scalar(wcol[:, :], ps_m[:, 0:1], br_sb[:, 0:1], None, ALU.add).then_inc(d0["w"], 1)
                dve.wait_ge(d0["w"], b + 1)
                dve.tensor_copy(wts[:, bass.ds(b, 1)], wcol[:, :]).then_inc(d0["wts"], 1)
                dve.wait_ge(d0["y"], b + 1)
                dve.tensor_tensor(y1[:, :], ps_y[:, 0:D], b2_sb[:, :], ALU.add).then_inc(d0["y1"], 1)
                dve.wait_ge(d0["y1"], b + 1)
                dve.tensor_scalar(blk, y1[:, :].rearrange("p (k c) -> p k c", k=KD), wcol[:, 0:1], None,
                                  ALU.mult).then_inc(d0["yw"], 1)

            with dve.If(early_flag0(dve)):
                for s in range(SLOTS):
                    prepare(0, s)
                group(0)
                group(1)
                dve.wait_ge(l0["acc"][SLOTS - 1], 2)
                block0(0)
                with dve.Fori(2, STEPS - 1) as i:
                    group(i)
                    dve.wait_ge(l0["acc"][SLOTS - 1], i + 1)
                    block0(i - 1)
                for s in range(SLOTS):
                    add_window(STEPS - 1, s)
                dve.wait_ge(l0["acc"][SLOTS - 1], STEPS)
                block0(STEPS - 2)
                block0(STEPS - 1)
            with dve.Else():
                all_windows()
                block0(0)
                with dve.Fori(1, BLOCKS) as b:
                    block0(b)

            steps = [0]

            def then(ins):
                steps[0] += 1
                ins.then_inc(q_v, 1)
                dve.wait_ge(q_v, steps[0])

            dve.wait_ge(d0["wts"], BLOCKS)
            dve.wait_ge(d0["yw"], BLOCKS)
            bits = wts[:, :].bitcast(I32)
            then(dve.tensor_scalar(key[:, 0, :], bits, 31, -2147483648, ALU.arith_shift_right, ALU.bitwise_or))
            then(dve.tensor_tensor(key[:, 1, :], bits, key[:, 0, :], ALU.bitwise_xor))
            then(dve.tensor_scalar(key[:, 2, :], key[:, 1, :], 16, 0xffff, ALU.logical_shift_right, ALU.bitwise_and))
            then(dve.tensor_scalar(key[:, 3, :], key[:, 1, :], 0xffff, None, ALU.bitwise_and))
            HI, LO, V, EQ, GT, VALID, TMP, NODE = range(8)
            then(dve.tensor_copy(kf[:, HI, :], key[:, 2, :]))
            then(dve.tensor_copy(kf[:, LO, :], key[:, 3, :]))
            then(dve.tensor_scalar(kf[:, VALID, :], kf[:, NODE, :], float(N), None, ALU.is_lt))
            then(dve.scalar_tensor_tensor(out=kf[:, TMP, :], in0=kf[:, HI, :], scalar=1.0, in1=kf[:, VALID, :],
                                          op0=ALU.add, op1=ALU.mult))
            then(dve.tensor_scalar(kf[:, HI, :], kf[:, TMP, :], -1.0, None, ALU.add))
            BITS = 16
            counted = [0]

            def total(col_in):
                counted[0] += 1
                dve.wait_ge(q_mm, counted[0])

            def search(values, into):
                cand, step = srch[:, 0:1], srch[:, 1:2]
                then(dve.memset(cand, float(2 ** (BITS - 1))))
                for k in range(BITS - 1, -1, -1):
                    then(dve.tensor_scalar(kf[:, TMP, :], values, cand, None, ALU.is_ge))
                    then(dve.tensor_reduce(cnt[:, :], kf[:, TMP, :], AX_X, ALU.add))
                    total(cnt)
                    then(dve.tensor_scalar(step, ps_m[:, 0:1], float(KEEP), float(2 ** k), ALU.is_ge, ALU.mult))
                    nxt = -float(2 ** k) + (float(2 ** (k - 1)) if k else 0.0)
                    then(dve.tensor_scalar(cand if k else into, cand, step, None, ALU.add))
                    then(dve.tensor_scalar(cand if k else into, cand if k else into, nxt, None, ALU.add))

            search(kf[:, HI, :], srch[:, 2:3])
            then(dve.tensor_scalar(kf[:, GT, :], kf[:, HI, :], srch[:, 2:3], 65536.0, ALU.is_gt, ALU.mult))
            then(dve.tensor_scalar(kf[:, EQ, :], kf[:, HI, :], srch[:, 2:3], None, ALU.is_equal))
            then(dve.scalar_tensor_tensor(out=kf[:, V, :], in0=kf[:, LO, :], scalar=1.0, in1=kf[:, EQ, :],
                                          op0=ALU.add, op1=ALU.mult))
            then(dve.scalar_tensor_tensor(out=kf[:, V, :], in0=kf[:, V, :], scalar=-1.0, in1=kf[:, GT, :],
                                          op0=ALU.add, op1=ALU.add))
            search(kf[:, V, :], srch[:, 3:4])
            then(dve.tensor_scalar(kf[:, GT, :], kf[:, V, :], srch[:, 3:4], None, ALU.is_gt))
            then(dve.tensor_reduce(cnt[:, :], kf[:, GT, :], AX_X, ALU.add))
            total(cnt)
            then(dve.tensor_scalar(srch[:, 4:5], ps_m[:, 0:1], -1.0, float(KEEP), ALU.mult, ALU.add))
            then(dve.tensor_scalar(kf[:, EQ, :], kf[:, V, :], srch[:, 3:4], None, ALU.is_equal))
            total(None)
            then(dve.tensor_copy(kf[:, TMP, :], ps_m[:, P:P + BLOCKS]))
            then(dve.tensor_tensor_scan(kf[:, LO, :], kf[:, TMP, :], zero49[:, :], 0.0, ALU.add, ALU.add))
            then(dve.tensor_tensor(kf[:, LO, :], kf[:, LO, :], kf[:, TMP, :], ALU.subtract))
            then(dve.tensor_tensor(kf[:, LO, :], kf[:, LO, :], ps_m[:, 2 * P:2 * P + BLOCKS], ALU.add))
            then(dve.tensor_scalar(kf[:, TMP, :], kf[:, LO, :], srch[:, 4:5], None, ALU.is_lt))
            then(dve.tensor_tensor(kf[:, TMP, :], kf[:, TMP, :], kf[:, EQ, :], ALU.mult))
            then(dve.tensor_tensor(sel[:, :], kf[:, TMP, :], kf[:, GT, :], ALU.add))

            for t in range(BATCHES):
                bb, hb = bbuf[t % 2], hbuf[t % 2]
                dve.wait_ge(m_in[t % 2], 16 * (t // 2 + 1))
                if t >= 2:
                    dve.wait_ge(m_out[t % 2], 32 * (t // 2))
                for m in range(MB):
                    b = t * MB + m
                    dve.scalar_tensor_tensor(
                        out=bb[:, m, :].rearrange("p (k c) -> p k c", k=KD),
                        in0=acc[:, :, b * P:(b + 1) * P], scalar=sel[:, b:b + 1],
                        in1=bb[:, m, :].rearrange("p (k c) -> p k c", k=KD), op0=ALU.mult,
                        op1=ALU.add).then_inc(m_x2, 1)
                if t >= 1:
                    dve.wait_ge(m_h, MB * t)
                for m in range(MB):
                    dve.wait_ge(m_x2, t * MB + m + 1)
                    dve.bn_stats(st6[:, m, :], bb[:, m, :]).then_inc(m_bs, 1)
                for m in range(MB):
                    dve.wait_ge(m_bs, t * MB + m + 1)
                    dve.bn_aggr(mv[:, m, :], st6[:, m, :]).then_inc(m_mv, 1)
                dve.wait_ge(m_std, t + 1)
                dve.reciprocal(rstd[:, :], std[:, :]).then_inc(m_rstd, 1)
                dve.wait_ge(m_rstd, t + 1)
                for m in range(MB):
                    dve.tensor_scalar(hb[:, m, :], bb[:, m, :], mv[:, m, 0:1], rstd[:, m:m + 1],
                                      ALU.subtract, ALU.mult).then_inc(m_h, 1)
            dve.memset(acc[:, :, :], 0.0).then_inc(s_ra, 1)
            dve.wait_ge(s_ra, 2)

            def block1(b):
                blk = acc[:, :, bass.ds(b * P, P)]
                psT = ps_t[:, 0:D].rearrange("p (k c) -> p k c", k=KD)
                dve.wait_ge(d1["tr1"], b + 1)
                wait(dve, d1["g"], b)
                dve.tensor_tensor(addT[:, :].rearrange("p (k c) -> p k c", k=KD), psT, blk,
                                  ALU.add).then_inc(d1["add"], 1)
                dve.tensor_tensor(mulT[:, :].rearrange("p (k c) -> p k c", k=KD), psT, blk,
                                  ALU.mult).then_inc(d1["mul"], 1)
                dve.wait_ge(d1["g"], b + 1)
                wait(dve, d1["out"], 16 * b)
                dve.tensor_tensor(z[:, :], ps_y[:, :], gb_sb[:, :, :].rearrange("p a d -> p (a d)"),
                                  ALU.add).then_inc(d1["z"], 1)
                dve.wait_ge(d1["z"], b + 1)
                dve.scalar_tensor_tensor(out=z[:, :], in0=z[:, :], scalar=0.01, in1=z[:, :], op0=ALU.mult,
                                         op1=ALU.max).then_inc(d1["zl"], 1)
                dve.wait_ge(d1["zl"], b + 1)
                dve.tensor_tensor(y1[:, :], z[:, D:2 * D], z[:, 0:D], ALU.add).then_inc(d1["zs"], 1)
                dve.wait_ge(d1["zs"], b + 1)
                dve.wait_ge(d1["x_in"], 16 * (b + 1))
                dve.tensor_tensor(x3[:, :], y1[:, :], xb[:, :], ALU.add).then_inc(d1["x3"], 1)
                dve.wait_ge(d1["x3"], b + 1)
                block_norm(d1, b, x3[:, :], h[:, :])
                n = [0]

                def gate(ins):
                    n[0] += 1
                    ins.then_inc(d1["gate"], 1)
                    dve.wait_ge(d1["gate"], GATE_STEPS * b + n[0])

                G, M1, OH1, G2, M2, OH2, C1, C = (g8[:, j, :] for j in range(8))
                V0, R1, V1, R2, DL, DEN, G1, G2W = (gs[:, j:j + 1] for j in range(8))
                dve.wait_ge(d1["lg"], b + 1)
                gate(dve.tensor_tensor(G, ps_m[:, 0:EXPERTS], gsum_sb[:, :], ALU.add))
                gate(dve.tensor_reduce(V0, G, AX_X, ALU.max))
                gate(dve.scalar_tensor_tensor(out=M1, in0=G, scalar=V0, in1=desc[:, :], op0=ALU.is_equal,
                                              op1=ALU.mult))
                gate(dve.tensor_reduce(R1, M1, AX_X, ALU.max))
                gate(dve.tensor_scalar(OH1, desc[:, :], R1, None, ALU.is_equal))
                gate(dve.scalar_tensor_tensor(out=G2, in0=OH1, scalar=-BIG, in1=G, op0=ALU.mult, op1=ALU.add))
                gate(dve.tensor_reduce(V1, G2, AX_X, ALU.max))
                gate(dve.scalar_tensor_tensor(out=M2, in0=G2, scalar=V1, in1=desc[:, :], op0=ALU.is_equal,
                                              op1=ALU.mult))
                gate(dve.tensor_reduce(R2, M2, AX_X, ALU.max))
                gate(dve.tensor_scalar(OH2, desc[:, :], R2, None, ALU.is_equal))
                gate(dve.tensor_tensor(DL, V1, V0, ALU.subtract))
                dve.wait_ge(d1["exp"], b + 1)
                gate(dve.tensor_scalar(DEN, ex[:, :], 1.0, None, ALU.add))
                gate(dve.reciprocal(G1, DEN))
                gate(dve.tensor_tensor(G2W, G1, ex[:, :], ALU.mult))
                gate(dve.tensor_scalar(C1, OH1, G1, None, ALU.mult))
                gate(dve.scalar_tensor_tensor(out=C, in0=OH2, scalar=G2W, in1=C1, op0=ALU.mult, op1=ALU.add))
                assert n[0] == GATE_STEPS
                dve.wait_ge(d1["ct"], b + 1)
                dve.tensor_copy(cTs[:, :], ps_m[0:EXPERTS, P:2 * P]).then_inc(d1["cts"], 1)
                dve.wait_ge(d1["b2"], b + 1)
                dve.tensor_tensor(o, x3[:, :], ps_m[:, D:2 * D], ALU.add).then_inc(d1["o0"], 1)
                dve.wait_ge(d1["o0"], b + 1)
                for e in range(EXPERTS):
                    dve.wait_ge(d1["y"], EXPERTS * b + e + 1)
                    wait(dve, d1["o"], EXPERTS * b + e)
                    dve.scalar_tensor_tensor(out=o, in0=ps_y2[e % 2][:, 0:D],
                                             scalar=g8[:, 7, e:e + 1], in1=o, op0=ALU.mult,
                                             op1=ALU.add).then_inc(d1["o"], 1)

            def prepare_records(i, s):
                wait(dve, b_in[s], 16 * (i + 1))
                if not isinstance(i, int) or i > 0:
                    dve.wait_ge(b_mm, 2 * BSLOTS * (i - 1) + 2 * s + 2)
                for t in range(BG):
                    ins = dve.tensor_scalar(bonehot[:, s, t, :], iota_w[:, :], rec_in[:, s, t, 1:2].bitcast(F32),
                                            rec_in[:, s, t, 2:3].bitcast(F32), ALU.is_equal, ALU.mult)
                ins.then_inc(b_oh[s], 1)

            def add_tiles(i, u):
                for t in range(BG // 2):
                    m = STEP_TILES * i + BG // 2 * u + t
                    at = dve.value_load(window_of[0:1, bass.ds(m, 1)], min_val=0, max_val=NPAD - WIN)
                    if t == 0:
                        dve.wait_ge(b_mm, 2 * BSLOTS * i + u + 1)
                    wait(dve, b_add, m)
                    cols = acc[:, :, bass.ds(at, WIN)]
                    dve.tensor_tensor(cols, cols, ps_seg[u % 2][:, t * KD * WIN:(t + 1) * KD * WIN]
                                      .rearrange("p (k w) -> p k w", k=KD), ALU.add).then_inc(b_add, 1)

            def add_slot(i, s):
                add_tiles(i, 2 * s)
                add_tiles(i, 2 * s + 1)

            def record_group(i):
                for s in range(BSLOTS):
                    add_slot(i, s)
                    prepare_records(i + 1, s)
                dve.wait_ge(b_add, STEP_TILES * (i + 1))

            dve.wait_ge(c_wback, 16)
            for s in range(BSLOTS):
                prepare_records(0, s)
            for s in range(BSLOTS):
                add_slot(0, s)
                prepare_records(1, s)
            dve.wait_ge(b_add, STEP_TILES)
            with dve.If(early_flag1(dve)):
                with dve.Fori(1, LAG + 1) as i:
                    record_group(i)
                block1(0)
                with dve.Fori(LAG + 1, LAG + BLOCKS) as i:
                    record_group(i)
                    block1(i - LAG)
                for s in range(BSLOTS):
                    add_slot(BSTEPS - 1, s)
            with dve.Else():
                with dve.Fori(1, BSTEPS - 1) as i:
                    record_group(i)
                for s in range(BSLOTS):
                    add_slot(BSTEPS - 1, s)
                dve.wait_ge(b_add, STEP_TILES * BSTEPS)
                block1(0)
                with dve.Fori(1, BLOCKS) as b:
                    block1(b)

        @block.scalar
        def _(act):
            def std_a(b):
                act.wait_ge(a_mv, b + 1)
                hold(act)
                act.activation(std[:, 0:1], mv[:, 0, 1:2], ACT.Sqrt, bias=eps_c[:, 0:1]).then_inc(a_std, 1)

            def copy_hT(b, q):
                act.wait_ge(a_tr, b + 1)
                wait(act, a_ch, T_CHUNKS * (b - 1))
                hold(act)
                act.activation(hT[:, q, :], ps_t[:, 0:D], ACT.Copy).then_inc(a_hT, 1)

            def evict(b, q, times):
                for c in range(1, T_CHUNKS, 2):
                    act.wait_ge(a_ch, T_CHUNKS * b + c + 1)
                    if c == 1:
                        wait(act, a_out[q], 16 * times)
                    hold(act)
                    act.activation(tbuf[q][:, c * CH:(c + 1) * CH], t_banks[c % 4][:, :],
                                   ACT.Copy).then_inc(a_ev_s, 1)
                act.wait_ge(a_ev_v, 4 * b + 4 + 2)
                act.wait_ge(a_ev_s, 4 * b + 4 + 2)
                act.dma_start(table0_rows[bass.ds(b * P, P), :], tbuf[q]).then_inc(a_out[q], 16)

            act.wait_ge(s_kv, 3)
            std_a(0)
            copy_hT(0, 0)
            std_a(1)
            copy_hT(1, 1)
            evict(0, 0, 0)
            std_a(2)
            copy_hT(2, 0)
            evict(1, 1, 0)
            with act.Fori(1, BLOCKS // 2) as j:
                std_a(2 * j + 1)
                copy_hT(2 * j + 1, 1)
                evict(2 * j, 0, j)
                std_a(2 * j + 2)
                copy_hT(2 * j + 2, 0)
                evict(2 * j + 1, 1, j)
            evict(BLOCKS - 1, 0, BLOCKS // 2)
            act.wait_ge(s_c, 16 * N_CONSTS)

            def block_std(v, b):
                act.wait_ge(v["mv"], b + 1)
                hold(act)
                act.activation(std[:, 0:1], mv[:, 0, 1:2], ACT.Sqrt, bias=eps_c[:, 0:1]).then_inc(v["std"], 1)

            def block_hT(v, b, used, uses):
                act.wait_ge(v["trH"], b + 1)
                wait(act, v[used], uses * b)
                hold(act)
                act.activation(hT[:, 0, :], ps_t[:, D:2 * D], ACT.Copy).then_inc(v["hT"], 1)

            def block0(b):
                block_std(d0, b)
                block_hT(d0, b, "hid", 2)
                wait(act, d0["y"], b)
                for q in range(2):
                    act.wait_ge(d0["hid"], 2 * b + q + 1)
                    hold(act)
                    for c in range(4 * q, 4 * q + 4):
                        act.activation(hid[:, c * P:(c + 1) * P], ps_h[q][:, (c % 4) * P:(c % 4 + 1) * P],
                                       ACT.Gelu_apprx_tanh, bias=b1_sb[:, c:c + 1]).then_inc(d0["gelu"], 1)
                act.wait_ge(d0["base"], b + 1)
                act.dma_start(base_d[bass.ds(b * P, P), :], base[:, :]).then_inc(d0["out"], 16)

            def block1(b):
                block_std(d1, b)
                block_hT(d1, b, "hid", EXPERTS)
                act.wait_ge(d1["gate"], GATE_STEPS * b + 11)
                hold(act)
                act.activation(ex[:, :], gs[:, 4:5], ACT.Exp).then_inc(d1["exp"], 1)
                for e in range(EXPERTS):
                    act.wait_ge(d1["hid"], EXPERTS * b + e + 1)
                    if e >= 2:
                        act.wait_ge(d1["y"], EXPERTS * b + e - 1)
                    else:
                        wait(act, d1["y"], EXPERTS * b)
                    hold(act)
                    for c in range(EC):
                        ins = act.activation(hid[:, (e % 2) * EHID + c * P:(e % 2) * EHID + (c + 1) * P],
                                             ps_h[e % 2][:, c * P:(c + 1) * P], ACT.Relu,
                                             bias=eb1_sb[:, e * EC + c:e * EC + c + 1])
                    ins.then_inc(d1["relu"], 1)
                act.wait_ge(d1["o"], EXPERTS * (b + 1))
                act.dma_start(out[bass.ds(b * P, P), :], o).then_inc(d1["out"], 16)

            def layer(block_work):
                block_work(0)
                with act.Fori(1, BLOCKS) as b:
                    block_work(b)

            layer(block0)
            for t in range(BATCHES):
                act.wait_ge(m_mv, MB * (t + 1))
                act.activation(std[:, :], mv[:, :, 1], ACT.Sqrt, bias=eps_c[:, 0:1]).then_inc(m_std, 1)
            layer(block1)

        @block.tensor
        def _(pe):
            pe.wait_ge(s_k, 12)
            pe.wait_ge(s_kv, 3)

            def transpose_block(src, dst, done):
                for k in range(KD):
                    ins = pe.transpose(dst[:, k * P:(k + 1) * P], src[:, k * P:(k + 1) * P], ident[:, :])
                ins.then_inc(done, 1)

            def count_pass(i, first, last):
                for k, (t0, n) in enumerate(SPLITS):
                    pe.wait_ge(c_ob1, NSPLIT * i + k + 1)
                    pe.matmul(ps_count[:, 0:n * WINDOWS], ones_bf[:, :],
                              inb[:, t0:t0 + n, :].rearrange("p t b -> p (t b)"),
                              start=(first and k == 0), stop=(last and k == NSPLIT - 1)).then_inc(c_mm1, 1)

            count_pass(0, True, False)
            with pe.Fori(1, BLOCKS - 1) as i:
                count_pass(i, False, False)
            count_pass(BLOCKS - 1, False, True)
            for r in range(4):
                pe.wait_ge(c_cmp, r + 1)
                wait(pe, c_win, r)
                pe.matmul(ps_count[:, 0:BTILES // 4], ones_bf[0:WINDOWS, :],
                          inb[:, :, :].rearrange("p t b -> p (t b)")[0:WINDOWS, 0:BTILES // 4],
                          start=True, stop=True).then_inc(c_mm1, 1)

            def transpose_a(b):
                pe.wait_ge(a_h, b + 1)
                wait(pe, a_hT, b)
                transpose_block(h, ps_t, a_tr)

            def rank_split(i, k):
                t0, n = SPLITS[k]
                pe.wait_ge(c_ob, NSPLIT * i + k + 1)
                wait(pe, c_take, 3 * (NSPLIT * i + k))

                def tiles(a, b):
                    return inb[:, t0 + a:t0 + b, :].rearrange("p t b -> p (t b)")

                for d in range(1, n):
                    pe.matmul(ps_place[:, d * WINDOWS:n * WINDOWS], ones_bf[:, :], tiles(0, n - d),
                              start=(d == 1), stop=False, skip_group_check=True)
                pe.matmul(ps_place[:, 0:n * WINDOWS], before_bf[:, :], tiles(0, n), start=False, stop=True,
                          skip_group_check=True)
                for t in range(n):
                    ins = pe.matmul(ps_tot[:, 0:WINDOWS], ones_bf[:, :], tiles(t, t + 1), start=(t == 0),
                                    stop=(t == n - 1))
                ins.then_inc(c_mm, 1)

            def table_and_ranks(b, q):
                pe.wait_ge(a_hT, b + 1)
                for c in range(T_CHUNKS):
                    pe.wait_ge((a_ev_v, a_ev_s)[c % 2], 4 * b + c // 2 + 1)
                    for k in range(KD):
                        ins = pe.matmul(t_banks[c % 4][:, :], hT[:, q, k * P:(k + 1) * P],
                                        wrel_sb[:, k, c * CH:(c + 1) * CH], start=(k == 0), stop=(k == KD - 1))
                    ins.then_inc(a_ch, 1)
                    if c < NSPLIT:
                        rank_split(b, c)

            transpose_a(0)
            pe.wait_ge(s_w, 32)
            transpose_a(1)
            table_and_ranks(0, 0)
            transpose_a(2)
            table_and_ranks(1, 1)
            with pe.Fori(1, BLOCKS // 2) as j:
                transpose_a(2 * j + 1)
                table_and_ranks(2 * j, 0)
                transpose_a(2 * j + 2)
                table_and_ranks(2 * j + 1, 1)
            table_and_ranks(BLOCKS - 1, 0)
            pe.wait_ge(c_take, 3 * NSPLIT * BLOCKS)
            pe.wait_ge(a_ev_v, 4 * BLOCKS + 2)
            pe.wait_ge(a_ev_s, 4 * BLOCKS + 2)
            pe.wait_ge(s_c, 16 * N_CONSTS)

            def sum_window(s, done):
                for k in range(KD):
                    for t in range(TG):
                        ins = pe.matmul(ps_seg[s][:, k * WIN:(k + 1) * WIN], ring[:, s, t, k * P:(k + 1) * P],
                                        onehot[:, s, t, :], start=(t == 0), stop=(t == TG - 1))
                ins.then_inc(done, 1)

            def group(i):
                for s in range(SLOTS):
                    pe.wait_ge(l0["rows"][s], 16 * TG * (i + 1))
                    pe.wait_ge(l0["oh"][s], i + 1)
                    wait(pe, l0["acc"][s], i)
                    sum_window(s, l0["mm"][s])

            def all_windows():
                with pe.Fori(0, GROUPS) as g:
                    pe.wait_ge(l0["rows"][0], 16 * TG * (g + 1))
                    hold(pe)
                    with pe.Fori(0, WINDOWS) as w:
                        pe.wait_ge(l0["goh"], g * WINDOWS + w + 1)
                        pe.wait_ge(l0["gacc"], g * WINDOWS + w + 1)
                        sum_window(0, l0["gmm"])

            def block0(b):
                pe.wait_ge(d0["accs"], b + 1)
                wait(pe, d0["w"], b)
                transpose_block(accs, ps_t[:, 0:D], d0["trA"])
                pe.wait_ge(d0["h"], b + 1)
                wait(pe, d0["hT"], b)
                transpose_block(h, ps_t[:, D:2 * D], d0["trH"])
                pe.wait_ge(d0["hT"], b + 1)
                for k in range(KD):
                    ins = pe.matmul(ps_m[:, 0:1], hT[:, 0, k * P:(k + 1) * P], wr_sb[:, k:k + 1],
                                    start=(k == 0), stop=(k == KD - 1))
                ins.then_inc(d0["rt"], 1)
                wait(pe, d0["gelu"], HC * b)
                for q in range(2):
                    for c in range(4 * q, 4 * q + 4):
                        for k in range(KD):
                            ins = pe.matmul(ps_h[q][:, (c % 4) * P:(c % 4 + 1) * P],
                                            w1_sb[:, k, c * P:(c + 1) * P], hT[:, 0, k * P:(k + 1) * P],
                                            start=(k == 0), stop=(k == KD - 1))
                    ins.then_inc(d0["hid"], 1)
                wait(pe, d0["y1"], b)
                for c in range(HC):
                    pe.wait_ge(d0["gelu"], HC * b + c + 1)
                    ins = pe.matmul(ps_y[:, 0:D], hid[:, c * P:(c + 1) * P], w2_sb[:, c, :],
                                    start=(c == 0), stop=(c == HC - 1))
                ins.then_inc(d0["y"], 1)

            def block1(b):
                pe.wait_ge(d1["h_in"], 16 * (b + 1))
                wait(pe, d1["o0"], b)
                transpose_block(hin, ps_t[:, 0:D], d1["tr1"])
                pe.wait_ge(d1["mul"], b + 1)
                wait(pe, d1["o"], EXPERTS * b)
                for a, left in enumerate((addT, mulT)):
                    for k in range(KD):
                        ins = pe.matmul(ps_y[:, a * D:(a + 1) * D], left[:, k * P:(k + 1) * P],
                                        gw_sb[:, a, k, :], start=(k == 0), stop=(k == KD - 1))
                ins.then_inc(d1["g"], 1)
                pe.wait_ge(d1["h"], b + 1)
                wait(pe, d1["hT"], b)
                transpose_block(h, ps_t[:, D:2 * D], d1["trH"])
                pe.wait_ge(d1["hT"], b + 1)
                for k in range(KD):
                    ins = pe.matmul(ps_m[:, 0:EXPERTS], hT[:, 0, k * P:(k + 1) * P], wg_sb[:, k, :],
                                    start=(k == 0), stop=(k == KD - 1))
                ins.then_inc(d1["lg"], 1)

                def hidden(e):
                    wait(pe, d1["relu"], EXPERTS * b + e - 1 if e >= 2 else EXPERTS * b)
                    for c in range(EC):
                        for k in range(KD):
                            ins = pe.matmul(ps_h[e % 2][:, c * P:(c + 1) * P],
                                            ew1_sb[:, e, k, c * P:(c + 1) * P], hT[:, 0, k * P:(k + 1) * P],
                                            start=(k == 0), stop=(k == KD - 1))
                    ins.then_inc(d1["hid"], 1)

                def outputs(e):
                    pe.wait_ge(d1["relu"], EXPERTS * b + e + 1)
                    if e >= 2:
                        pe.wait_ge(d1["o"], EXPERTS * b + e - 1)
                    for c in range(EC):
                        ins = pe.matmul(ps_y2[e % 2][:, 0:D],
                                        hid[:, (e % 2) * EHID + c * P:(e % 2) * EHID + (c + 1) * P],
                                        ew2_sb[:, e, c, :], start=(c == 0), stop=(c == EC - 1))
                    ins.then_inc(d1["y"], 1)

                hidden(0)
                hidden(1)
                pe.wait_ge(d1["gate"], GATE_STEPS * (b + 1))
                pe.transpose(ps_m[0:EXPERTS, P:2 * P], g8[:, 7, :], ident[:, :]).then_inc(d1["ct"], 1)
                outputs(0)
                pe.wait_ge(d1["cts"], b + 1)
                pe.matmul(ps_m[:, D:2 * D], cTs[:, :], eb2_sb[:, :], start=True, stop=True).then_inc(d1["b2"], 1)
                for e in range(2, EXPERTS):
                    hidden(e)
                    outputs(e - 1)
                outputs(EXPERTS - 1)

            both_ways0(pe, early_flag0(pe), group, all_windows, block0)

            step = [9]
            done = 0
            for half in range(2):
                step[0] += 1
                for k in range(16):
                    step[0] += 2
                    pe.wait_ge(q_v, step[0])
                    pe.matmul(ps_m[:, 0:1], ones[:, :], cnt[:, :], start=True, stop=True).then_inc(q_mm, 1)
                    step[0] += 3
                step[0] += 4 if half == 0 else 2
            pe.wait_ge(q_v, step[0])
            pe.matmul(ps_m[:, 0:1], ones[:, :], cnt[:, :], start=True, stop=True).then_inc(q_mm, 1)
            pe.wait_ge(q_v, step[0] + 2)
            pe.matmul(ps_m[:, P:P + BLOCKS], ones[:, :], kf[:, 3, :], start=True, stop=True)
            pe.matmul(ps_m[:, 2 * P:2 * P + BLOCKS], before[:, :], kf[:, 3, :], start=True,
                      stop=True).then_inc(q_mm, 1)

            pe.wait_ge(s_ew, 32)
            pe.wait_ge(s_kv, 7)

            def record_group(i):
                for u in range(2 * BSLOTS):
                    s = u // 2
                    if u % 2 == 0:
                        pe.wait_ge(b_rows[s], 16 * BG * (i + 1))
                        pe.wait_ge(b_oh[s], i + 1)
                    wait(pe, b_add, max(0, BG // 2 * (u - 1)) if isinstance(i, int) and i == 0
                         else STEP_TILES * i + BG // 2 * (u - 1))
                    for t in range(BG // 2):
                        for k in range(KD):
                            ins = pe.matmul(ps_seg[u % 2][:, (t * KD + k) * WIN:(t * KD + k + 1) * WIN],
                                            bring[:, s, u % 2 * BG // 2 + t, k * P:(k + 1) * P],
                                            bonehot[:, s, u % 2 * BG // 2 + t, :], start=True, stop=True)
                    ins.then_inc(b_mm, 1)

            both_ways1(pe, early_flag1(pe), record_group, block1)


def kernel(**inputs):
    import numpy as np
    import concourse.bacc as bacc
    from concourse import mybir as _mybir
    from concourse.bass_utils import run_bass_kernel_spmd

    def a(name):
        return np.ascontiguousarray(inputs[name])

    def padded(v, n, fill):
        return np.concatenate([v, np.full((n - v.shape[0],) + v.shape[1:], fill, v.dtype)])

    def by_group(v, fill):
        return np.ascontiguousarray(padded(v, EPAD, fill).reshape(GROUPS, TG, P).transpose(0, 2, 1))

    def by_lane(v):
        return np.ascontiguousarray(v.transpose(1, 0, 2).reshape(P, LANE_TILES))

    src, rel, dst = (by_group(a(n), f) for n, f in (("src", 0), ("edge_type_16", 0), ("dst", N - 1)))
    arrays = {
        "x": padded(a("x"), NPAD, 0),
        "edge_ints": np.ascontiguousarray(np.concatenate([src, rel, dst], axis=2)),
        "dst_lanes": by_lane(dst), "src_lanes": by_lane(src),
        "norm0": by_group(a("edge_weight1").reshape(E), 0),
        "norm1_lanes": by_lane(by_group(a("edge_weight"), 0)),
        "wrel": np.ascontiguousarray(a("L0_gnn_weight").reshape(RELS, KD, P, D).transpose(1, 2, 0, 3)),
        "wr": np.ascontiguousarray(a("L0_ffn_wr").reshape(KD, P).T),
        "br": a("L0_ffn_br"),
        "w1": a("L0_ffn_w1"), "b1": np.ascontiguousarray(a("L0_ffn_b1").reshape(HC, P).T),
        "w2": a("L0_ffn_w2"), "b2": a("L0_ffn_b2"),
        "gw1t": np.ascontiguousarray(a("L1_gnn_W1").T), "gb1": a("L1_gnn_b1"),
        "gw2t": np.ascontiguousarray(a("L1_gnn_W2").T), "gb2": a("L1_gnn_b2"),
        "wg": a("L1_ffn_Wg"), "bg": a("L1_ffn_bg"), "gbias": a("L1_ffn_bias"),
        "ew1": a("L1_ffn_W1"),
        "eb1": np.ascontiguousarray(a("L1_ffn_b1").reshape(EXPERTS * EC, P).T),
        "ew2": a("L1_ffn_W2"), "eb2": a("L1_ffn_b2"),
    }
    nc = bacc.Bacc("TRN2", target_bir_lowering=False, num_devices=1)
    args = {n: nc.dram_tensor(f"in_{n}", v.shape, _mybir.dt.from_np(v.dtype), kind="ExternalInput").ap()
            for n, v in arrays.items()}
    args["out"] = nc.dram_tensor("out_x", (NPAD, D), _mybir.dt.float32, kind="ExternalOutput").ap()
    gnn_kernel(nc, **args)
    r = run_bass_kernel_spmd(nc, [{f"in_{n}": v for n, v in arrays.items()}], core_ids=[0])
    return r.results[0]["out_x"][:N]
```

```python
from contextlib import ExitStack

import concourse.bass as bass
from concourse import mybir

ALU = mybir.AluOpType
ACT = mybir.ActivationFunctionType
F32 = mybir.dt.float32
I32 = mybir.dt.int32
BF16 = mybir.dt.bfloat16
AX_X = mybir.AxisListType.X

P = 128
N = 6250
D = 256
E = 206250
RELS = 16
HIDDEN = 1024
EXPERTS, EHID = 8, 512
BLOCKS = -(-N // P)
NPAD = BLOCKS * P
KD = D // P
TG = 11
SLOTS = 3
STEP_EDGES = SLOTS * TG * P
STEPS = -(-E // STEP_EDGES)
GROUPS = STEPS * SLOTS
EPAD = STEPS * STEP_EDGES
WIN = 64
WINDOWS = NPAD // WIN
ACC_COLS = NPAD + WIN
CH = 512
T_CHUNKS = RELS * D // CH
PER_CHUNK = CH // D
HC = HIDDEN // P
EC = EHID // P
KEEP = max(1, N // 2) - 1
LANE_TILES = GROUPS * TG
PASS_TILES = SLOTS * TG
BATCH = CH // WINDOWS
SIZES = [BATCH, PASS_TILES % BATCH] + [BATCH] * (PASS_TILES // BATCH - 1)
SPLITS = [(sum(SIZES[:k]), n) for k, n in enumerate(SIZES)]
NSPLIT = len(SPLITS)
BG, BSLOTS = 8, 4
STEP_TILES = BG * BSLOTS
UNITS = 8
UTILES = STEP_TILES // UNITS
LAG = 5
BSTEPS = 54
BTILES = BSTEPS * STEP_TILES
REC = 3
MB = 7
BATCHES = BLOCKS // MB
assert UNITS == EXPERTS and UNITS == 2 * BSLOTS
EPS = 1e-5
BIG = 1e30
GATE_STEPS = 16
assert BTILES >= LANE_TILES + WINDOWS and BSTEPS == BLOCKS + LAG
assert STEPS == BLOCKS and BLOCKS % 2 == 1 and BLOCKS % MB == 0


def gnn_kernel(nc, x, edge_ints, dst_lanes, src_lanes, norm0, norm1_lanes, wrel, wr, br, w1, b1, w2, b2,
               gw1t, gb1, gw2t, gb2, wg, bg, gbias, ew1, eb1, ew2, eb2, out):
    table0 = nc.dram_tensor("table0", (NPAD * RELS, D), F32, kind="Internal").ap()
    table1 = nc.dram_tensor("table1", (NPAD, D), F32, kind="Internal").ap()
    base_d = nc.dram_tensor("base_d", (NPAD, D), F32, kind="Internal").ap()
    x2_d = nc.dram_tensor("x2_d", (NPAD, D), F32, kind="Internal").ap()
    records = nc.dram_tensor("records", ((BTILES + STEP_TILES) * P, REC), I32, kind="Internal").ap()
    windows_d = nc.dram_tensor("windows_d", (1, BTILES), I32, kind="Internal").ap()
    table0_rows = table0.rearrange("(n r) d -> n (r d)", r=RELS)

    ctx = ExitStack()
    with ctx:
        def sb(name, shape, dt=F32):
            return ctx.enter_context(nc.sbuf_tensor(name, shape, dt))

        def pb(name):
            return ctx.enter_context(nc.psum_tensor(name, [P, CH], F32))

        def sem(name):
            return ctx.enter_context(nc.semaphore(name))

        acc = sb("acc", [P, KD, ACC_COLS])
        arena = sb("arena", [P, 2 * EXPERTS * KD * EHID])
        wrel_sb = arena[:, 0:RELS * KD * D].rearrange("p (k n) -> p k n", k=KD)
        tbuf = [arena[:, (2 + q) * RELS * D:(3 + q) * RELS * D] for q in range(2)]
        ew1_sb = arena[:, 0:EXPERTS * KD * EHID].rearrange("p (e k n) -> p e k n", e=EXPERTS, k=KD)
        ew2_sb = arena[:, EXPERTS * KD * EHID:].rearrange("p (e c n) -> p e c n", e=EXPERTS, c=EC)
        ring = sb("ring", [P, SLOTS, TG, D])
        ringf = ring[:, :, :, :].rearrange("p s t d -> p (s t d)")
        dst_all = ringf[:, 0:GROUPS * TG].bitcast(I32)
        bbuf = [ringf[:, q * MB * D:(q + 1) * MB * D].rearrange("p (m d) -> p m d", m=MB) for q in range(2)]
        hbuf = [ringf[:, (2 + q) * MB * D:(3 + q) * MB * D].rearrange("p (m d) -> p m d", m=MB) for q in range(2)]
        accf = acc[:, :, :].rearrange("p k n -> p (k n)")
        at = [0]

        def borrow(n, dt=F32):
            at[0] += n
            assert at[0] <= KD * ACC_COLS
            v = accf[:, at[0] - n:at[0]]
            return v if dt == F32 else v.bitcast(dt)

        zeros_rec = borrow(BTILES * REC)
        src_all = borrow(LANE_TILES, I32)
        rel_i = borrow(LANE_TILES, I32)
        wt_all = borrow(LANE_TILES)
        bkt = borrow(LANE_TILES // 2 + 1).bitcast(BF16)
        rel_bf = borrow(LANE_TILES // 2 + 1).bitcast(BF16)
        iota_b = sb("iota_b", [P, WINDOWS], BF16)
        ones_bf = sb("ones_bf", [P, P], BF16)
        before_bf = sb("before_bf", [P, P], BF16)
        carry = sb("carry", [P, WINDOWS])
        bcount = sb("bcount", [P, 4, WINDOWS])
        bcount_i = sb("bcount_i", [P, WINDOWS], I32)
        pos = sb("pos", [P, PASS_TILES])
        addr = sb("addr", [P, 4, PASS_TILES], I32)
        place_i = sb("place_i", [P, 2, PASS_TILES], I32)
        rec_out = sb("rec_out", [P, 2, PASS_TILES, REC], I32)
        bflag = sb("bflag", [P, 1], I32)
        onehot_all = sb("onehot", [P, SLOTS * TG * WIN])
        onehot = onehot_all[:, :].rearrange("p (s t w) -> p s t w", s=SLOTS, t=TG)
        bonehot = onehot_all[:, 0:STEP_TILES * WIN].rearrange("p (s t w) -> p s t w", s=BSLOTS, t=BG)
        inb = onehot_all[:, 0:PASS_TILES * WINDOWS // 2].bitcast(BF16).rearrange("p (t b) -> p t b", b=WINDOWS)
        bring = ringf[:, 0:STEP_TILES * D].rearrange("p (s t d) -> p s t d", s=BSLOTS, t=BG)
        rec_in = sb("rec_in", [P, BSLOTS, BG, REC], I32)
        eint = sb("eint", [P, SLOTS, 3, TG], I32)
        ewt = sb("ewt", [P, SLOTS, TG])
        idx = sb("idx", [P, SLOTS, TG], I32)
        drel = sb("drel", [P, SLOTS, TG])
        w1_sb = sb("w1_sb", [P, KD, HIDDEN])
        w2_sb = sb("w2_sb", [P, HC, D])
        b1_sb = sb("b1_sb", [P, HC])
        b2_sb = sb("b2_sb", [P, D])
        wr_sb = sb("wr_sb", [P, KD])
        br_sb = sb("br_sb", [P, 1])
        gw_sb = sb("gw_sb", [P, 2, KD, D])
        gb_sb = sb("gb_sb", [P, 2, D])
        wg_sb = sb("wg_sb", [P, KD, EXPERTS])
        gbias_sb = sb("gbias_sb", [P, 2, EXPERTS])
        gsum_sb = sb("gsum_sb", [P, EXPERTS])
        eb1_sb = sb("eb1_sb", [P, EXPERTS * EC])
        eb2_sb = sb("eb2_sb", [EXPERTS, D])
        ident = sb("ident", [P, P])
        ones = sb("ones", [P, P])
        before = sb("before", [P, P])
        iota_w = sb("iota_w", [P, WIN])
        wbase = sb("wbase", [P, WINDOWS])
        desc = sb("desc", [P, EXPERTS])
        eps_c = sb("eps_c", [P, 1])
        zero49 = sb("zero49", [P, BLOCKS])
        span = borrow(2 * GROUPS).rearrange("p (a g) -> p a g", a=2)
        spanr = borrow(2 * GROUPS).rearrange("p (a g) -> p a g", a=2)
        gmin = sb("gmin", [P, GROUPS])
        gmin_i = sb("gmin_i", [P, GROUPS], I32)
        gdiff = borrow(2 * GROUPS).rearrange("p (a g) -> p a g", a=2)
        earliest = sb("earliest", [P, GROUPS])
        worst = sb("worst", [P, 2])
        fits = sb("fits", [P, 2])
        flag = sb("flag", [P, 1], I32)
        xa = sb("xa", [P, 2, D])
        st6 = sb("st6", [P, MB, 6])
        mv = sb("mv", [P, MB, 2])
        std = sb("std", [P, MB])
        rstd = sb("rstd", [P, MB])
        h = sb("h", [P, D])
        xb = sb("xb", [P, D])
        hT = sb("hT", [P, 2, KD * P])
        accs = sb("accs", [P, KD * P])
        base = sb("base", [P, D])
        hid = sb("hid", [P, HC * P])
        y1 = sb("y1", [P, D])
        wcol = sb("wcol", [P, 1])
        wts = sb("wts", [P, BLOCKS])
        z = sb("z", [P, 2 * D])
        placed = z[:, 0:BATCH * WINDOWS].rearrange("p (t b) -> p t b", b=WINDOWS)
        window_made = ringf[0:1, 2048:2048 + BTILES].bitcast(I32)
        window_of = w1_sb[:, :, :].rearrange("p k n -> p (k n)")[0:1, 0:BTILES].bitcast(I32)
        hin, x3, addT, mulT = xa[:, 0, :], xa[:, 1, :], accs, base
        g8 = sb("g8", [P, 8, EXPERTS])
        gs = sb("gs", [P, 8])
        cTs = sb("cTs", [EXPERTS, P])
        ex = sb("ex", [P, 1])
        w2f = w2_sb[:, :, :].rearrange("p c n -> p (c n)")
        o, first_o, gates = w2f[:, 0:D], w2f[:, D:2 * D], w2f[:, 2 * D:2 * D + EXPERTS]
        key = y1[:, 0:4 * BLOCKS].bitcast(I32).rearrange("p (a b) -> p a b", a=4)
        kf = sb("kf", [P, 8, BLOCKS])
        sel = sb("sel", [P, BLOCKS])
        cnt = sb("cnt", [P, 1])
        srch = sb("srch", [P, 8])

        ps_seg = [pb(f"ps_seg{s}") for s in range(SLOTS)]
        ps_t = pb("ps_t")
        ps_m = ps_t
        ps_y2 = [pb("ps_y0"), pb("ps_y1")]
        ps_y = ps_y2[0]
        ps_g = ps_seg[2]
        ps_h = [pb("ps_h0"), pb("ps_h1")]
        ps_count, ps_place, ps_tot = ps_y2[0], ps_h[1], ps_y2[1]
        t_banks = [ps_seg[0], ps_seg[1], ps_seg[2], ps_h[0]]

        s_w = sem("s_wrel_in")
        s_c = sem("s_consts_in")
        N_CONSTS = 16
        s_dst = sem("s_dst_in")
        s_ew = sem("s_expert_weights_in")
        s_k = sem("s_iotas")
        s_kv = sem("s_consts_made")
        s_span, s_spanr, s_win = sem("s_span"), sem("s_span_all"), sem("s_windows")
        s_ra = sem("s_acc_zero")
        a_x = [sem(f"a_x_in{q}") for q in range(2)]
        a_st, a_mv, a_std, a_rstd, a_h = (sem(f"a_{n}") for n in ("stats", "meanvar", "std", "rstd", "h"))
        a_tr, a_hT, a_ch = (sem(f"a_{n}") for n in ("transposed", "hT", "chunk"))
        a_ev_v, a_ev_s = sem("a_evicted_v"), sem("a_evicted_s")
        a_out = [sem(f"a_table_out{q}") for q in range(2)]
        seg = []
        for L in range(1):
            seg.append({
                "in": [sem(f"l{L}_edges_in{s}") for s in range(SLOTS)],
                "idx": [sem(f"l{L}_idx{s}") for s in range(SLOTS)],
                "rel": [sem(f"l{L}_rel{s}") for s in range(SLOTS)],
                "oh": [sem(f"l{L}_onehots{s}") for s in range(SLOTS)],
                "rows": [sem(f"l{L}_rows_in{s}") for s in range(SLOTS)],
                "mm": [sem(f"l{L}_window_summed{s}") for s in range(SLOTS)],
                "acc": [sem(f"l{L}_window_added{s}") for s in range(SLOTS)],
                "goh": sem(f"l{L}_all_onehots"), "gmm": sem(f"l{L}_all_summed"), "gacc": sem(f"l{L}_all_added"),
            })
        l0 = seg[0]
        c_rows, c_zero, c_zeroed = sem("c_rows_in"), sem("c_zeros_made"), sem("c_records_zeroed")
        c_pre, c_ob1, c_mm1 = sem("c_buckets"), sem("c_count_onehots"), sem("c_counted")
        c_end, c_cmp, c_win = sem("c_bucket_ends"), sem("c_tile_compared"), sem("c_tile_windows")
        c_wout, c_wback = sem("c_windows_out"), sem("c_windows_back")
        c_bflag = sem("c_bflag")
        c_ob, c_mm, c_take = sem("c_onehots"), sem("c_ranked"), sem("c_placed")
        c_addr, c_rec = sem("c_addresses"), sem("c_records")
        c_out = [sem(f"c_scattered{q}") for q in range(2)]
        b_in, b_oh, b_rows = ([sem(f"b_{n}{s}") for s in range(BSLOTS)] for n in ("records", "onehots", "rows"))
        b_mm, b_add = sem("b_summed"), sem("b_added")
        d0 = {n: sem(f"d0_{n}") for n in
              ("accs", "trA", "x_in", "x1", "bs", "mv", "std", "rstd", "h", "base", "out", "trH", "hT", "rt",
               "w", "wts", "hid", "gelu", "y", "y1", "yw")}
        q_v, q_mm = sem("select_step"), sem("select_counted")
        m_in = [sem(f"m_base_in{q}") for q in range(2)]
        m_out = [sem(f"m_out{q}") for q in range(2)]
        m_x2, m_bs, m_mv, m_std, m_rstd, m_h = (sem(f"m_{n}") for n in ("x2", "bs", "mv", "std", "rstd", "h"))
        d1 = {n: sem(f"d1_{n}") for n in
              ("h_in", "x_in", "tr1", "add", "mul", "g", "z", "zl", "zs", "x3", "bs", "mv", "std", "rstd", "h",
               "trH", "hT", "hT2", "lg", "gate", "exp", "ct", "cts", "b2", "o0", "gates", "hid", "relu", "y", "o", "out")}

        block = ctx.enter_context(nc.Block())

        def wait(eng, signal, value):
            if not isinstance(value, int) or value > 0:
                eng.wait_ge(signal, value)

        def hold(eng):
            eng.nop(nofuse=True)

        def both_ways0(eng, early, group_work, window_work, block_work):
            with eng.If(early):
                group_work(0)
                group_work(1)
                block_work(0)
                with eng.Fori(2, STEPS) as i:
                    group_work(i)
                    block_work(i - 1)
                block_work(BLOCKS - 1)
            with eng.Else():
                window_work()
                block_work(0)
                with eng.Fori(1, BLOCKS) as b:
                    block_work(b)

        def both_ways1(eng, early, step):
            step(0, True, None, None)
            with eng.If(early):
                with eng.Fori(1, LAG) as i:
                    step(i, True, None, None)
                step(LAG, True, 0, None)
                step(LAG + 1, True, 1, 0)
                with eng.Fori(LAG + 2, BSTEPS) as i:
                    step(i, True, i - LAG, i - LAG - 1)
            with eng.Else():
                with eng.Fori(1, BSTEPS) as i:
                    step(i, True, None, None)
                step(None, False, 0, None)
                step(None, False, 1, 0)
                with eng.Fori(2, BLOCKS) as b:
                    step(None, False, b, b - 1)
            step(None, False, None, BLOCKS - 1)

        def early_flag0(eng):
            eng.wait_ge(s_win, 1)
            return eng.value_load(flag[0:1, 0:1], min_val=0, max_val=1)

        def early_flag1(eng):
            eng.wait_ge(c_bflag, 1)
            return eng.value_load(bflag[0:1, 0:1], min_val=0, max_val=1)

        @block.sync
        def _(sp):
            def load_x(b, q):
                wait(sp, a_h, b - 1)
                sp.dma_start(xa[:, q, :], x[bass.ds(b * P, P), :]).then_inc(a_x[q], 16)

            sp.dma_start(src_all, src_lanes).then_inc(c_rows, 16)
            sp.dma_start(dst_all, dst_lanes).then_inc(s_dst, 16)
            sp.dma_start(wt_all, norm1_lanes).then_inc(c_rows, 16)
            load_x(0, 0)
            load_x(1, 1)
            for k in range(KD):
                sp.dma_start(wrel_sb[:, k, :], wrel[k].rearrange("p r o -> p (r o)")).then_inc(s_w, 16)
            sp.wait_ge(c_zero, 1)
            sp.dma_start(records[0:BTILES * P, :].rearrange("(p n) r -> p (n r)", p=P),
                         zeros_rec.bitcast(I32)).then_inc(c_zeroed, 16)
            sp.dma_start(records[BTILES * P:, :].rearrange("(p n) r -> p (n r)", p=P),
                         zeros_rec[:, 0:STEP_TILES * REC].bitcast(I32)).then_inc(c_zeroed, 16)
            for dst, src in (
                (w1_sb[:, :, :], w1.rearrange("(k p) n -> p k n", p=P)),
                (w2_sb[:, :, :], w2.rearrange("(c p) n -> p c n", p=P)),
                (b1_sb[:, :], b1), (b2_sb[:, :], b2.partition_broadcast(P)),
                (wr_sb[:, :], wr), (br_sb[:, :], br.partition_broadcast(P)),
                (gw_sb[:, 0, :, :], gw1t.rearrange("(k p) n -> p k n", p=P)),
                (gw_sb[:, 1, :, :], gw2t.rearrange("(k p) n -> p k n", p=P)),
                (gb_sb[:, 0, :], gb1.partition_broadcast(P)), (gb_sb[:, 1, :], gb2.partition_broadcast(P)),
                (wg_sb[:, 0, :], wg[0:P, :]), (wg_sb[:, 1, :], wg[P:D, :]),
                (gbias_sb[:, 0, :], bg.partition_broadcast(P)), (gbias_sb[:, 1, :], gbias.partition_broadcast(P)),
                (eb1_sb[:, :], eb1), (eb2_sb[:, :], eb2),
            ):
                sp.dma_start(dst, src).then_inc(s_c, 16)
            sp.wait_ge(c_win, 4)
            sp.dma_start(windows_d, window_made).then_inc(c_wout, 16)
            load_x(2, 0)
            with sp.Fori(1, BLOCKS // 2) as j:
                load_x(2 * j + 1, 1)
                load_x(2 * j + 2, 0)

            sp.wait_ge(a_ch, T_CHUNKS * BLOCKS)
            sp.wait_ge(a_out[0], 16 * (BLOCKS // 2 + 1))
            sp.wait_ge(a_out[1], 16 * (BLOCKS // 2))
            sp.dma_start(ew1_sb, ew1.rearrange("e (k p) n -> p e k n", p=P)).then_inc(s_ew, 16)
            sp.dma_start(ew2_sb, ew2.rearrange("e (c p) n -> p e c n", p=P)).then_inc(s_ew, 16)

            def load_edges(g, s):
                sp.dma_start(eint[:, s, :, :], edge_ints[bass.ds(g, 1), :, :]
                             .rearrange("g p n -> (g p) n")).then_inc(l0["in"][s], 16)
                sp.dma_start(ewt[:, s, :], norm0[bass.ds(g, 1), :, :]
                             .rearrange("g p n -> (g p) n")).then_inc(l0["in"][s], 16)

            def load_step(i):
                for s in range(SLOTS):
                    wait(sp, l0["oh"][s], i)
                    load_edges(SLOTS * i + s, s)

            def all_windows():
                load_edges(0, 0)
                with sp.Fori(1, GROUPS) as g:
                    sp.wait_ge(l0["gacc"], g * WINDOWS + 1)
                    load_edges(g, 0)

            def block0(b):
                wait(sp, d0["x1"], b)
                sp.dma_start(xb[:, :], x[bass.ds(b * P, P), :]).then_inc(d0["x_in"], 16)

            def block1(b):
                wait(sp, d1["tr1"], b)
                sp.dma_start(hin, table1[bass.ds(b * P, P), :]).then_inc(d1["h_in"], 16)
                wait(sp, d1["x3"], b)
                sp.dma_start(xb[:, :], x2_d[bass.ds(b * P, P), :]).then_inc(d1["x_in"], 16)

            with sp.If(early_flag0(sp)):
                load_step(0)
                load_step(1)
                block0(0)
                with sp.Fori(2, STEPS) as i:
                    load_step(i)
                    block0(i - 1)
                block0(BLOCKS - 1)
            with sp.Else():
                all_windows()
                block0(0)
                with sp.Fori(1, BLOCKS) as b:
                    block0(b)

            sp.wait_ge(d0["hid"], 2 * BLOCKS)
            sp.wait_ge(c_wout, 16)
            sp.dma_start(window_of, windows_d).then_inc(c_wback, 16)

            sp.wait_ge(d0["out"], 16 * BLOCKS)

            def rows(dram, t):
                return dram[bass.ds(t * MB * P, MB * P), :].rearrange("(m p) d -> p m d", p=P)

            for t in range(BATCHES + 1):
                if t < BATCHES:
                    if t >= 2:
                        sp.wait_ge(m_out[t % 2], 32 * (t // 2))
                    sp.dma_start(bbuf[t % 2], rows(base_d, t)).then_inc(m_in[t % 2], 16)
                if t >= 1:
                    sp.wait_ge(m_x2, MB * t)
                    sp.dma_start(rows(x2_d, t - 1), bbuf[(t - 1) % 2]).then_inc(m_out[(t - 1) % 2], 16)
                    sp.wait_ge(m_h, MB * t)
                    sp.dma_start(rows(table1, t - 1), hbuf[(t - 1) % 2]).then_inc(m_out[(t - 1) % 2], 16)

            def load_records(i, s):
                wait(sp, b_rows[s], 16 * BG * i)
                wait(sp, b_oh[s], i)
                sp.dma_start(rec_in[:, s, :, :].rearrange("p t r -> p (t r)"),
                             records[bass.ds((BSLOTS * i + s) * BG * P, BG * P), :]
                             .rearrange("(p t) r -> p (t r)", p=P)).then_inc(b_in[s], 16)

            def load_record_step(i):
                for s in range(BSLOTS):
                    load_records(i, s)

            sp.wait_ge(c_out[0], 16 * PASS_TILES * (BLOCKS // 2 + 1))
            sp.wait_ge(c_out[1], 16 * PASS_TILES * (BLOCKS // 2))
            load_record_step(0)
            sp.wait_ge(m_out[0], 32 * ((BATCHES + 1) // 2))
            sp.wait_ge(m_out[1], 32 * (BATCHES // 2))
            block1(0)
            with sp.If(early_flag1(sp)):
                with sp.Fori(1, LAG + 1) as i:
                    load_record_step(i)
                with sp.Fori(LAG + 1, BSTEPS) as i:
                    load_record_step(i)
                    block1(i - LAG)
            with sp.Else():
                with sp.Fori(1, BSTEPS) as i:
                    load_record_step(i)
                with sp.Fori(1, BLOCKS) as b:
                    block1(b)
            load_record_step(BSTEPS)
            sp.wait_ge(d1["out"], 16 * BLOCKS)

        @block.gpsimd
        def _(pool):
            pool.iota(iota_w[:, :], [[1, WIN]], base=0, channel_multiplier=0,
                      allow_small_or_imprecise_dtypes=True).then_inc(s_k, 1)
            pool.iota(wbase[:, :], [[WIN, WINDOWS]], base=0, channel_multiplier=0,
                      allow_small_or_imprecise_dtypes=True).then_inc(s_k, 1)
            pool.iota(desc[:, :], [[-1, EXPERTS]], base=EXPERTS, channel_multiplier=0,
                      allow_small_or_imprecise_dtypes=True).then_inc(s_k, 1)
            pool.iota(earliest[:, :], [[P, STEPS], [0, SLOTS]], base=-P, channel_multiplier=0,
                      allow_small_or_imprecise_dtypes=True).then_inc(s_k, 1)
            pool.iota(kf[:, 7, :], [[P, BLOCKS]], base=0, channel_multiplier=1,
                      allow_small_or_imprecise_dtypes=True).then_inc(s_k, 1)
            pool.iota(bcount[:, 0, :], [[1, WINDOWS]], base=0, channel_multiplier=0,
                      allow_small_or_imprecise_dtypes=True).then_inc(s_k, 1)
            pool.iota(z[:, 0:BTILES // 4], [[1, BTILES // 4]], base=0, channel_multiplier=0,
                      allow_small_or_imprecise_dtypes=True).then_inc(s_k, 1)
            pool.iota(kf[:, 6, :], [[STEP_TILES, BLOCKS]], base=STEP_TILES * LAG, channel_multiplier=0,
                      allow_small_or_imprecise_dtypes=True).then_inc(s_k, 1)
            pool.memset(ident[:, :], 0.0).then_inc(s_k, 1)
            pool.memset(before[:, :], 0.0).then_inc(s_k, 1)
            pool.wait_ge(s_k, 10)
            pool.affine_select(out=ident[:, :], in_=ident[:, :], compare_op=ALU.not_equal, fill=1.0, base=0,
                               pattern=[[-1, P]], channel_multiplier=1).then_inc(s_k, 1)
            pool.affine_select(out=before[:, :], in_=before[:, :], compare_op=ALU.is_ge, fill=1.0, base=0,
                               pattern=[[-1, P]], channel_multiplier=1).then_inc(s_k, 1)
            pool.wait_ge(s_span, 3)
            pool.partition_all_reduce(spanr[:, :, :].rearrange("p a g -> p (a g)"),
                                      span[:, :, :].rearrange("p a g -> p (a g)"), P,
                                      bass.bass_isa.ReduceOp.max).then_inc(s_spanr, 1)
            def scatter(i, q):
                wait(pool, c_rec, 4 * (i + 1))
                hold(pool)
                for t in range(PASS_TILES):
                    pool.indirect_dma_start(records, bass.IndirectOffsetOnAxis(ap=place_i[:, q, t:t + 1], axis=0),
                                            rec_out[:, q, t, :], None).then_inc(c_out[q], 16)

            pool.wait_ge(c_zeroed, 32)
            scatter(0, 0)
            with pool.Fori(0, BLOCKS // 2) as j:
                scatter(2 * j + 1, 1)
                scatter(2 * j + 2, 0)

            def gather(s):
                for t in range(TG):
                    pool.indirect_dma_start(ring[:, s, t, :], None, table0,
                                            bass.IndirectOffsetOnAxis(ap=idx[:, s, t:t + 1], axis=0)
                                            ).then_inc(l0["rows"][s], 16)

            def group(i):
                for s in range(SLOTS):
                    wait(pool, l0["idx"][s], i + 1)
                    wait(pool, l0["mm"][s], i)
                    hold(pool)
                    gather(s)

            def all_windows():
                with pool.Fori(0, GROUPS) as g:
                    pool.wait_ge(l0["idx"][0], g + 1)
                    pool.wait_ge(l0["gmm"], g * WINDOWS + 1)
                    hold(pool)
                    gather(0)

            pool.wait_ge(c_wout, 16)
            pool.wait_ge(a_out[0], 16 * (BLOCKS // 2 + 1))
            pool.wait_ge(a_out[1], 16 * (BLOCKS // 2))
            with pool.If(early_flag0(pool)):
                group(0)
                with pool.Fori(1, STEPS) as i:
                    group(i)
            with pool.Else():
                all_windows()

            def record_group(i):
                for s in range(BSLOTS):
                    wait(pool, b_in[s], 16 * (i + 1))
                    if not isinstance(i, int):
                        pool.wait_ge(b_mm, 2 * BSLOTS * (i - 1) + 2 * s + 2)
                    hold(pool)
                    for t in range(BG):
                        pool.indirect_dma_start(bring[:, s, t, :], None, table1,
                                                bass.IndirectOffsetOnAxis(ap=rec_in[:, s, t, 0:1], axis=0)
                                                ).then_inc(b_rows[s], 16)

            pool.wait_ge(m_out[0], 32 * ((BATCHES + 1) // 2))
            pool.wait_ge(m_out[1], 32 * (BATCHES // 2))
            record_group(0)
            with pool.Fori(1, BSTEPS) as i:
                record_group(i)

        @block.vector
        def _(dve):
            dve.memset(ones[:, :], 1.0).then_inc(s_kv, 1)
            dve.memset(eps_c[:, :], EPS).then_inc(s_kv, 1)
            dve.memset(zero49[:, :], 0.0).then_inc(s_kv, 1)
            dve.memset(zeros_rec, 0.0).then_inc(c_zero, 1)
            dve.memset(cnt[:, :], 0.0).then_inc(a_ev_v, 2)
            dve.memset(srch[:, :], 0.0).then_inc(a_ev_s, 2)
            dve.memset(ones_bf[:, :], 1.0).then_inc(s_kv, 1)
            dve.wait_ge(s_k, 12)
            dve.tensor_copy(before_bf[:, :], before[:, :]).then_inc(s_kv, 1)
            dve.tensor_copy(iota_b[:, :], bcount[:, 0, :]).then_inc(s_kv, 1)

            dve.wait_ge(c_rows, 32)
            dve.tensor_scalar(rel_i, src_all, WIN - 1, None, ALU.bitwise_and).then_inc(c_pre, 1)
            dve.wait_ge(c_pre, 1)
            dve.tensor_copy(rel_bf[:, 0:LANE_TILES], rel_i).then_inc(c_pre, 1)
            dve.wait_ge(c_pre, 2)
            dve.tensor_scalar(rel_i, src_all, WIN.bit_length() - 1, None, ALU.logical_shift_right).then_inc(c_pre, 1)
            dve.wait_ge(c_pre, 3)
            dve.tensor_copy(bkt[:, 0:LANE_TILES], rel_i).then_inc(c_pre, 1)
            dve.wait_ge(c_pre, 4)
            dve.wait_ge(s_kv, 6)

            def bucket_onehots(i, k, done):
                t0, n = SPLITS[k]
                dve.tensor_tensor(inb[:, t0:t0 + n, :], iota_b[:, :].unsqueeze(1).broadcast_to([P, n, WINDOWS]),
                                  bkt[:, bass.ds(PASS_TILES * i + t0, n)].unsqueeze(2).broadcast_to([P, n, WINDOWS]),
                                  ALU.is_equal).then_inc(done, 1)

            def count_pass(i):
                for k in range(NSPLIT):
                    if not isinstance(i, int):
                        dve.wait_ge(c_mm1, NSPLIT * (i - 1) + k + 1)
                    bucket_onehots(i, k, c_ob1)

            count_pass(0)
            with dve.Fori(1, BLOCKS) as i:
                count_pass(i)

            ends = [0]

            def link(ins):
                ends[0] += 1
                ins.then_inc(c_end, 1)
                dve.wait_ge(c_end, ends[0])

            dve.wait_ge(c_mm1, NSPLIT * BLOCKS)
            link(dve.tensor_reduce(bcount[:, 0, :], ps_count[:, 0:BATCH * WINDOWS]
                                   .rearrange("p (t b) -> p b t", b=WINDOWS), AX_X, ALU.add))
            link(dve.tensor_scalar(bcount[:, 0, :], bcount[:, 0, :], float(P - 1), None, ALU.add))
            link(dve.tensor_copy(bcount_i[:, :], bcount[:, 0, :]))
            link(dve.tensor_scalar(bcount_i[:, :], bcount_i[:, :], 7, None, ALU.logical_shift_right))
            link(dve.tensor_copy(bcount[:, 1, :], bcount_i[:, :]))
            link(dve.memset(bcount[:, 0, :], 0.0))
            link(dve.tensor_tensor_scan(bcount[:, 2, :], bcount[:, 1, :], bcount[:, 0, :], 0.0, ALU.add, ALU.add))
            link(dve.tensor_tensor(carry[:, :], bcount[:, 2, :], bcount[:, 1, :], ALU.subtract))
            link(dve.tensor_scalar(carry[:, :], carry[:, :], float(P), None, ALU.mult))
            link(dve.tensor_tensor(bcount[:, 3, :], bcount[:, 2, :], ident[:, 0:WINDOWS], ALU.mult))
            link(dve.tensor_reduce(cnt[:, :], bcount[:, 3, :], AX_X, ALU.add))
            quarter = BTILES // 4
            passed = inb[:, :, :].rearrange("p t b -> p (t b)")
            for r in range(4):
                wait(dve, c_win, r)
                dve.tensor_scalar(passed[0:WINDOWS, 0:quarter], z[0:WINDOWS, 0:quarter], float(r * quarter),
                                  cnt[0:WINDOWS, 0:1], ALU.add, ALU.is_ge).then_inc(c_cmp, 1)
                dve.wait_ge(c_mm1, NSPLIT * BLOCKS + r + 1)
                dve.tensor_scalar(window_made[0:1, r * quarter:(r + 1) * quarter], ps_count[0:1, 0:quarter],
                                  float(WINDOWS - 1), float(WIN), ALU.min, ALU.mult).then_inc(c_win, 1)
            ends_of_blocks = bcount[:, 2, :].rearrange("p (b two) -> p b two", two=2)[:, :, 1]
            link(dve.tensor_tensor(kf[:, 5, :], ends_of_blocks, kf[:, 6, :], ALU.subtract))
            link(dve.tensor_reduce(srch[:, 0:1], kf[:, 5, :], AX_X, ALU.max))
            dve.tensor_scalar(bflag[:, :], srch[:, 0:1], 0.0, None, ALU.is_le).then_inc(c_bflag, 1)

            dve.wait_ge(s_dst, 16)
            dstg = dst_all.rearrange("p (g t) -> p g t", t=TG)
            dve.tensor_reduce(gmin[:, :], dstg, AX_X, ALU.min).then_inc(s_span, 1)
            dve.tensor_reduce(span[:, 1, :], dstg, AX_X, ALU.max).then_inc(s_span, 1)
            dve.wait_ge(s_span, 1)
            dve.tensor_scalar(span[:, 0, :], gmin[:, :], -1.0, None, ALU.mult).then_inc(s_span, 1)
            dve.wait_ge(s_spanr, 1)
            dve.wait_ge(s_k, 12)
            dve.tensor_scalar(gmin[:, :], spanr[:, 0, :], -1.0, None, ALU.mult).then_inc(s_span, 1)
            dve.wait_ge(s_span, 4)
            dve.tensor_copy(gmin_i[:, :], gmin[:, :]).then_inc(s_span, 1)
            dve.tensor_tensor(gdiff[:, 0, :], spanr[:, 1, :], gmin[:, :], ALU.subtract).then_inc(s_span, 1)
            dve.tensor_tensor(gdiff[:, 1, :], earliest[:, :], gmin[:, :], ALU.subtract).then_inc(s_span, 1)
            dve.wait_ge(s_span, 7)
            dve.tensor_reduce(worst[:, :], gdiff[:, :, :], AX_X, ALU.max).then_inc(s_span, 1)
            dve.wait_ge(s_span, 8)
            dve.tensor_scalar(fits[:, 0:1], worst[:, 0:1], float(WIN - 1), None, ALU.is_le).then_inc(s_span, 1)
            dve.tensor_scalar(fits[:, 1:2], worst[:, 1:2], 0.0, None, ALU.is_le).then_inc(s_span, 1)
            dve.wait_ge(s_span, 10)
            dve.tensor_tensor(flag[:, :], fits[:, 0:1], fits[:, 1:2], ALU.mult).then_inc(s_win, 1)

            def norm_block(b, q, times):
                dve.wait_ge(a_x[q], 16 * times + 16)
                dve.bn_stats(st6[:, 0, :], xa[:, q, :]).then_inc(a_st, 1)
                dve.wait_ge(a_st, b + 1)
                hold(dve)
                dve.bn_aggr(mv[:, 0, :], st6[:, 0, :]).then_inc(a_mv, 1)
                dve.wait_ge(a_std, b + 1)
                dve.reciprocal(rstd[:, 0:1], std[:, 0:1]).then_inc(a_rstd, 1)
                dve.wait_ge(a_rstd, b + 1)
                wait(dve, a_tr, b)
                dve.tensor_scalar(h[:, :], xa[:, q, :], mv[:, 0, 0:1], rstd[:, 0:1],
                                  ALU.subtract, ALU.mult).then_inc(a_h, 1)

            def evict(b, q, times, c):
                dve.wait_ge(a_ch, T_CHUNKS * b + c + 1)
                if c == 0:
                    wait(dve, a_out[q], 16 * times)
                dve.tensor_copy(tbuf[q][:, c * CH:(c + 1) * CH], t_banks[c % 4][:, :]).then_inc(a_ev_v, 1)

            ADDR_STEPS = NSPLIT + 6

            def place_split(i, k):
                t0, n = SPLITS[k]
                m = NSPLIT * i + k
                dve.wait_ge(c_mm, m + 1)
                wait(dve, c_addr, ADDR_STEPS * i + k)
                dve.tensor_tensor(placed[:, 0:n, :], ps_place[:, 0:n * WINDOWS]
                                  .rearrange("p (t b) -> p t b", b=WINDOWS),
                                  carry[:, :].unsqueeze(1).broadcast_to([P, n, WINDOWS]),
                                  ALU.add).then_inc(c_take, 1)
                dve.wait_ge(c_take, 3 * m + 1)
                dve.tensor_tensor(placed[:, 0:n, :], placed[:, 0:n, :], inb[:, t0:t0 + n, :],
                                  ALU.mult).then_inc(c_take, 1)
                dve.tensor_tensor(carry[:, :], carry[:, :], ps_tot[:, 0:WINDOWS], ALU.add).then_inc(c_take, 1)
                dve.wait_ge(c_take, 3 * m + 3)
                dve.tensor_reduce(pos[:, t0:t0 + n], placed[:, 0:n, :], AX_X, ALU.add).then_inc(c_addr, 1)

            def finish_pass(i, q, times):
                n = [NSPLIT]

                def link(ins):
                    n[0] += 1
                    ins.then_inc(c_addr, 1)
                    dve.wait_ge(c_addr, ADDR_STEPS * i + n[0])

                dve.wait_ge(c_addr, ADDR_STEPS * i + NSPLIT)
                link(dve.tensor_copy(addr[:, 0, :], pos[:, :]))
                link(dve.tensor_scalar(addr[:, 1, :], addr[:, 0, :], -BG * P, None, ALU.bitwise_and))
                link(dve.tensor_scalar(addr[:, 2, :], addr[:, 0, :], P - 1, BG.bit_length() - 1,
                                       ALU.bitwise_and, ALU.logical_shift_left))
                link(dve.tensor_scalar(addr[:, 3, :], addr[:, 0, :], P.bit_length() - 1, BG - 1,
                                       ALU.logical_shift_right, ALU.bitwise_and))
                link(dve.tensor_tensor(addr[:, 1, :], addr[:, 1, :], addr[:, 2, :], ALU.bitwise_or))
                wait(dve, c_out[q], 16 * PASS_TILES * times)
                link(dve.tensor_copy(addr[:, 2, :], addr[:, 3, :]))
                assert n[0] == ADDR_STEPS
                dve.tensor_tensor(place_i[:, q, :], addr[:, 1, :], addr[:, 3, :],
                                  ALU.bitwise_or).then_inc(c_rec, 1)
                tiles = bass.ds(PASS_TILES * i, PASS_TILES)
                dve.tensor_copy(rec_out[:, q, :, 0], dst_all[:, tiles]).then_inc(c_rec, 1)
                dve.tensor_copy(rec_out[:, q, :, 1].bitcast(F32), rel_bf[:, tiles]).then_inc(c_rec, 1)
                dve.tensor_copy(rec_out[:, q, :, 2].bitcast(F32), wt_all[:, tiles]).then_inc(c_rec, 1)

            def table_and_places(b, q, times):
                bucket_onehots(b, 0, c_ob)
                for c in range(T_CHUNKS):
                    if c + 1 < NSPLIT:
                        bucket_onehots(b, c + 1, c_ob)
                    if c % 2 == 0:
                        evict(b, q, times, c)
                    if c < NSPLIT:
                        place_split(b, c)
                finish_pass(b, q, times)

            norm_block(0, 0, 0)
            norm_block(1, 1, 0)
            table_and_places(0, 0, 0)
            norm_block(2, 0, 1)
            table_and_places(1, 1, 0)
            with dve.Fori(1, BLOCKS // 2) as j:
                norm_block(2 * j + 1, 1, j)
                table_and_places(2 * j, 0, j)
                norm_block(2 * j + 2, 0, j + 1)
                table_and_places(2 * j + 1, 1, j)
            table_and_places(BLOCKS - 1, 0, BLOCKS // 2)
            dve.wait_ge(s_c, 16 * N_CONSTS)
            dve.tensor_tensor(gsum_sb[:, :], gbias_sb[:, 0, :], gbias_sb[:, 1, :], ALU.add).then_inc(s_kv, 1)
            dve.wait_ge(c_zeroed, 32)
            dve.wait_ge(c_rec, 4 * BLOCKS)
            dve.memset(acc[:, :, :], 0.0).then_inc(s_ra, 1)
            dve.wait_ge(s_ra, 1)

            def make_idx(s):
                dve.scalar_tensor_tensor(out=idx[:, s, :], in0=eint[:, s, 0, :], scalar=float(RELS),
                                         in1=eint[:, s, 1, :], op0=ALU.mult,
                                         op1=ALU.add).then_inc(l0["idx"][s], 1)

            def prepare(i, s):
                wait(dve, l0["in"][s], 32 * (i + 1))
                wait(dve, l0["rows"][s], 16 * TG * i)
                make_idx(s)
                dve.tensor_scalar(drel[:, s, :], eint[:, s, 2, :], gmin[:, bass.ds(SLOTS * i + s, 1)], None,
                                  ALU.subtract).then_inc(l0["rel"][s], 1)
                wait(dve, l0["rel"][s], i + 1)
                wait(dve, l0["mm"][s], i)
                for t in range(TG):
                    ins = dve.tensor_scalar(onehot[:, s, t, :], iota_w[:, :], drel[:, s, t:t + 1],
                                            ewt[:, s, t:t + 1], ALU.is_equal, ALU.mult)
                ins.then_inc(l0["oh"][s], 1)

            def add_window(i, s):
                at = dve.value_load(gmin_i[0:1, bass.ds(SLOTS * i + s, 1)], min_val=0, max_val=N - 1)
                wait(dve, l0["mm"][s], i + 1)
                wait(dve, l0["acc"][(s - 1) % SLOTS], i + (s > 0))
                cols = acc[:, :, bass.ds(at, WIN)]
                dve.tensor_tensor(cols, cols, ps_seg[s][:, 0:KD * WIN].rearrange("p (k w) -> p k w", k=KD),
                                  ALU.add).then_inc(l0["acc"][s], 1)

            def group(i):
                for s in range(SLOTS):
                    add_window(i, s)
                    prepare(i + 1, s)

            def all_windows():
                dve.memset(cnt[:, :], 0.0).then_inc(l0["gmm"], 1)
                dve.memset(srch[:, :], 0.0).then_inc(l0["gacc"], 1)
                with dve.Fori(0, GROUPS) as g:
                    dve.wait_ge(l0["in"][0], 32 * (g + 1))
                    dve.wait_ge(l0["gmm"], g * WINDOWS + 1)
                    make_idx(0)
                    with dve.Fori(0, WINDOWS) as w:
                        k = g * WINDOWS + w
                        dve.wait_ge(l0["gmm"], k + 1)
                        dve.tensor_scalar(drel[:, 0, :], eint[:, 0, 2, :], wbase[:, bass.ds(w, 1)], None,
                                          ALU.subtract).then_inc(l0["rel"][0], 1)
                        dve.wait_ge(l0["rel"][0], k + 1)
                        for t in range(TG):
                            ins = dve.tensor_scalar(onehot[:, 0, t, :], iota_w[:, :], drel[:, 0, t:t + 1],
                                                    ewt[:, 0, t:t + 1], ALU.is_equal, ALU.mult)
                        ins.then_inc(l0["goh"], 1)
                        dve.wait_ge(l0["gmm"], k + 2)
                        dve.wait_ge(l0["gacc"], k + 1)
                        cols = acc[:, :, bass.ds(w * WIN, WIN)]
                        dve.tensor_tensor(cols, cols,
                                          ps_seg[0][:, 0:KD * WIN].rearrange("p (k w) -> p k w", k=KD),
                                          ALU.add).then_inc(l0["gacc"], 1)
                dve.wait_ge(l0["gacc"], GROUPS * WINDOWS + 1)

            def norm_stats(v, b, src):
                dve.bn_stats(st6[:, 0, :], src).then_inc(v["bs"], 1)
                dve.wait_ge(v["bs"], b + 1)
                hold(dve)
                dve.bn_aggr(mv[:, 0, :], st6[:, 0, :]).then_inc(v["mv"], 1)

            def norm_apply(v, b, src, to):
                dve.wait_ge(v["std"], b + 1)
                dve.reciprocal(rstd[:, 0:1], std[:, 0:1]).then_inc(v["rstd"], 1)
                dve.wait_ge(v["rstd"], b + 1)
                wait(dve, v["trH"], b)
                dve.tensor_scalar(to, src, mv[:, 0, 0:1], rstd[:, 0:1],
                                  ALU.subtract, ALU.mult).then_inc(v["h"], 1)

            def block0(b):
                blk = acc[:, :, bass.ds(b * P, P)]
                wait(dve, d0["trA"], b)
                dve.tensor_copy(accs[:, :].rearrange("p (k c) -> p k c", k=KD), blk).then_inc(d0["accs"], 1)
                dve.wait_ge(d0["trA"], b + 1)
                dve.wait_ge(d0["x_in"], 16 * (b + 1))
                wait(dve, d0["base"], b)
                dve.tensor_tensor(z[:, 0:D], ps_t[:, 0:D], xb[:, :], ALU.add).then_inc(d0["x1"], 1)
                dve.wait_ge(d0["x1"], b + 1)
                norm_stats(d0, b, z[:, 0:D])
                norm_apply(d0, b, z[:, 0:D], h[:, :])
                dve.wait_ge(d0["h"], b + 1)
                wait(dve, d0["out"], 16 * b)
                dve.tensor_tensor(base[:, :], z[:, 0:D], h[:, :], ALU.add).then_inc(d0["base"], 1)
                dve.wait_ge(d0["rt"], b + 1)
                wait(dve, d0["yw"], b)
                dve.tensor_scalar(wcol[:, :], ps_m[:, 0:1], br_sb[:, 0:1], None, ALU.add).then_inc(d0["w"], 1)
                dve.wait_ge(d0["w"], b + 1)
                dve.tensor_copy(wts[:, bass.ds(b, 1)], wcol[:, :]).then_inc(d0["wts"], 1)
                dve.wait_ge(d0["y"], b + 1)
                dve.tensor_tensor(y1[:, :], ps_y[:, 0:D], b2_sb[:, :], ALU.add).then_inc(d0["y1"], 1)
                dve.wait_ge(d0["y1"], b + 1)
                dve.tensor_scalar(blk, y1[:, :].rearrange("p (k c) -> p k c", k=KD), wcol[:, 0:1], None,
                                  ALU.mult).then_inc(d0["yw"], 1)

            with dve.If(early_flag0(dve)):
                for s in range(SLOTS):
                    prepare(0, s)
                group(0)
                group(1)
                dve.wait_ge(l0["acc"][SLOTS - 1], 2)
                block0(0)
                with dve.Fori(2, STEPS - 1) as i:
                    group(i)
                    dve.wait_ge(l0["acc"][SLOTS - 1], i + 1)
                    block0(i - 1)
                for s in range(SLOTS):
                    add_window(STEPS - 1, s)
                dve.wait_ge(l0["acc"][SLOTS - 1], STEPS)
                block0(STEPS - 2)
                block0(STEPS - 1)
            with dve.Else():
                all_windows()
                block0(0)
                with dve.Fori(1, BLOCKS) as b:
                    block0(b)

            steps = [0]

            def then(ins):
                steps[0] += 1
                ins.then_inc(q_v, 1)
                dve.wait_ge(q_v, steps[0])

            dve.wait_ge(d0["wts"], BLOCKS)
            dve.wait_ge(d0["yw"], BLOCKS)
            bits = wts[:, :].bitcast(I32)
            then(dve.tensor_scalar(key[:, 0, :], bits, 31, -2147483648, ALU.arith_shift_right, ALU.bitwise_or))
            then(dve.tensor_tensor(key[:, 1, :], bits, key[:, 0, :], ALU.bitwise_xor))
            then(dve.tensor_scalar(key[:, 2, :], key[:, 1, :], 16, 0xffff, ALU.logical_shift_right, ALU.bitwise_and))
            then(dve.tensor_scalar(key[:, 3, :], key[:, 1, :], 0xffff, None, ALU.bitwise_and))
            HI, LO, V, EQ, GT, VALID, TMP, NODE = range(8)
            then(dve.tensor_copy(kf[:, HI, :], key[:, 2, :]))
            then(dve.tensor_copy(kf[:, LO, :], key[:, 3, :]))
            then(dve.tensor_scalar(kf[:, VALID, :], kf[:, NODE, :], float(N), None, ALU.is_lt))
            then(dve.scalar_tensor_tensor(out=kf[:, TMP, :], in0=kf[:, HI, :], scalar=1.0, in1=kf[:, VALID, :],
                                          op0=ALU.add, op1=ALU.mult))
            then(dve.tensor_scalar(kf[:, HI, :], kf[:, TMP, :], -1.0, None, ALU.add))
            BITS = 16
            counted = [0]

            def total(col_in):
                counted[0] += 1
                dve.wait_ge(q_mm, counted[0])

            def search(values, into):
                cand, step = srch[:, 0:1], srch[:, 1:2]
                then(dve.memset(cand, float(2 ** (BITS - 1))))
                for k in range(BITS - 1, -1, -1):
                    then(dve.tensor_scalar(kf[:, TMP, :], values, cand, None, ALU.is_ge))
                    then(dve.tensor_reduce(cnt[:, :], kf[:, TMP, :], AX_X, ALU.add))
                    total(cnt)
                    then(dve.tensor_scalar(step, ps_m[:, 0:1], float(KEEP), float(2 ** k), ALU.is_ge, ALU.mult))
                    nxt = -float(2 ** k) + (float(2 ** (k - 1)) if k else 0.0)
                    then(dve.tensor_scalar(cand if k else into, cand, step, None, ALU.add))
                    then(dve.tensor_scalar(cand if k else into, cand if k else into, nxt, None, ALU.add))

            search(kf[:, HI, :], srch[:, 2:3])
            then(dve.tensor_scalar(kf[:, GT, :], kf[:, HI, :], srch[:, 2:3], 65536.0, ALU.is_gt, ALU.mult))
            then(dve.tensor_scalar(kf[:, EQ, :], kf[:, HI, :], srch[:, 2:3], None, ALU.is_equal))
            then(dve.scalar_tensor_tensor(out=kf[:, V, :], in0=kf[:, LO, :], scalar=1.0, in1=kf[:, EQ, :],
                                          op0=ALU.add, op1=ALU.mult))
            then(dve.scalar_tensor_tensor(out=kf[:, V, :], in0=kf[:, V, :], scalar=-1.0, in1=kf[:, GT, :],
                                          op0=ALU.add, op1=ALU.add))
            search(kf[:, V, :], srch[:, 3:4])
            then(dve.tensor_scalar(kf[:, GT, :], kf[:, V, :], srch[:, 3:4], None, ALU.is_gt))
            then(dve.tensor_reduce(cnt[:, :], kf[:, GT, :], AX_X, ALU.add))
            total(cnt)
            then(dve.tensor_scalar(srch[:, 4:5], ps_m[:, 0:1], -1.0, float(KEEP), ALU.mult, ALU.add))
            then(dve.tensor_scalar(kf[:, EQ, :], kf[:, V, :], srch[:, 3:4], None, ALU.is_equal))
            total(None)
            then(dve.tensor_copy(kf[:, TMP, :], ps_m[:, P:P + BLOCKS]))
            then(dve.tensor_tensor_scan(kf[:, LO, :], kf[:, TMP, :], zero49[:, :], 0.0, ALU.add, ALU.add))
            then(dve.tensor_tensor(kf[:, LO, :], kf[:, LO, :], kf[:, TMP, :], ALU.subtract))
            then(dve.tensor_tensor(kf[:, LO, :], kf[:, LO, :], ps_m[:, 2 * P:2 * P + BLOCKS], ALU.add))
            then(dve.tensor_scalar(kf[:, TMP, :], kf[:, LO, :], srch[:, 4:5], None, ALU.is_lt))
            then(dve.tensor_tensor(kf[:, TMP, :], kf[:, TMP, :], kf[:, EQ, :], ALU.mult))
            then(dve.tensor_tensor(sel[:, :], kf[:, TMP, :], kf[:, GT, :], ALU.add))

            for t in range(BATCHES):
                bb, hb = bbuf[t % 2], hbuf[t % 2]
                dve.wait_ge(m_in[t % 2], 16 * (t // 2 + 1))
                if t >= 2:
                    dve.wait_ge(m_out[t % 2], 32 * (t // 2))
                for m in range(MB):
                    b = t * MB + m
                    dve.scalar_tensor_tensor(
                        out=bb[:, m, :].rearrange("p (k c) -> p k c", k=KD),
                        in0=acc[:, :, b * P:(b + 1) * P], scalar=sel[:, b:b + 1],
                        in1=bb[:, m, :].rearrange("p (k c) -> p k c", k=KD), op0=ALU.mult,
                        op1=ALU.add).then_inc(m_x2, 1)
                if t >= 1:
                    dve.wait_ge(m_h, MB * t)
                for m in range(MB):
                    dve.wait_ge(m_x2, t * MB + m + 1)
                    dve.bn_stats(st6[:, m, :], bb[:, m, :]).then_inc(m_bs, 1)
                for m in range(MB):
                    dve.wait_ge(m_bs, t * MB + m + 1)
                    dve.bn_aggr(mv[:, m, :], st6[:, m, :]).then_inc(m_mv, 1)
                dve.wait_ge(m_std, t + 1)
                dve.reciprocal(rstd[:, :], std[:, :]).then_inc(m_rstd, 1)
                dve.wait_ge(m_rstd, t + 1)
                for m in range(MB):
                    dve.tensor_scalar(hb[:, m, :], bb[:, m, :], mv[:, m, 0:1], rstd[:, m:m + 1],
                                      ALU.subtract, ALU.mult).then_inc(m_h, 1)
            dve.memset(acc[:, :, :], 0.0).then_inc(s_ra, 1)
            dve.wait_ge(s_ra, 2)

            def node_work(b, e):
                if e == 0:
                    blk = acc[:, :, bass.ds(b * P, P)]
                    psT = ps_t[:, 0:D].rearrange("p (k c) -> p k c", k=KD)
                    dve.wait_ge(d1["tr1"], b + 1)
                    wait(dve, d1["g"], b)
                    dve.tensor_tensor(addT[:, :].rearrange("p (k c) -> p k c", k=KD), psT, blk,
                                      ALU.add).then_inc(d1["add"], 1)
                    dve.tensor_tensor(mulT[:, :].rearrange("p (k c) -> p k c", k=KD), psT, blk,
                                      ALU.mult).then_inc(d1["mul"], 1)
                    dve.wait_ge(d1["mul"], b + 1)
                if e == 2:
                    dve.wait_ge(d1["g"], b + 1)
                    wait(dve, d1["zs"], b)
                    dve.tensor_tensor(z[:, :], ps_g[:, :], gb_sb[:, :, :].rearrange("p a d -> p (a d)"),
                                      ALU.add).then_inc(d1["z"], 1)
                    dve.wait_ge(d1["z"], b + 1)
                    dve.scalar_tensor_tensor(out=z[:, :], in0=z[:, :], scalar=0.01, in1=z[:, :], op0=ALU.mult,
                                             op1=ALU.max).then_inc(d1["zl"], 1)
                    dve.wait_ge(d1["zl"], b + 1)
                    dve.tensor_tensor(y1[:, :], z[:, D:2 * D], z[:, 0:D], ALU.add).then_inc(d1["zs"], 1)
                    dve.wait_ge(d1["zs"], b + 1)
                    dve.wait_ge(d1["x_in"], 16 * (b + 1))
                    dve.tensor_tensor(x3, y1[:, :], xb[:, :], ALU.add).then_inc(d1["x3"], 1)
                    dve.wait_ge(d1["x3"], b + 1)
                    norm_stats(d1, b, x3)
                if e == 3:
                    norm_apply(d1, b, x3, h[:, :])
                if e == 5:
                    gates_a(b)
                if e == 6:
                    gates_b(b)
                if e == 7:
                    dve.wait_ge(d1["ct"], b + 1)
                    dve.tensor_copy(cTs[:, :], ps_m[0:EXPERTS, P:2 * P]).then_inc(d1["cts"], 1)

            def gate(b, n, ins):
                ins.then_inc(d1["gate"], 1)
                dve.wait_ge(d1["gate"], GATE_STEPS * b + n)

            G, M1, OH1, G2, M2, OH2, C1, C = (g8[:, j, :] for j in range(8))
            V0, R1, V1, R2, DL, DEN, G1, G2W = (gs[:, j:j + 1] for j in range(8))

            def gates_a(b):
                dve.wait_ge(d1["lg"], b + 1)
                gate(b, 1, dve.tensor_tensor(G, ps_m[:, 0:EXPERTS], gsum_sb[:, :], ALU.add))
                gate(b, 2, dve.tensor_reduce(V0, G, AX_X, ALU.max))
                gate(b, 3, dve.scalar_tensor_tensor(out=M1, in0=G, scalar=V0, in1=desc[:, :], op0=ALU.is_equal,
                                                    op1=ALU.mult))
                gate(b, 4, dve.tensor_reduce(R1, M1, AX_X, ALU.max))
                gate(b, 5, dve.tensor_scalar(OH1, desc[:, :], R1, None, ALU.is_equal))
                gate(b, 6, dve.scalar_tensor_tensor(out=G2, in0=OH1, scalar=-BIG, in1=G, op0=ALU.mult,
                                                    op1=ALU.add))
                gate(b, 7, dve.tensor_reduce(V1, G2, AX_X, ALU.max))
                gate(b, 8, dve.scalar_tensor_tensor(out=M2, in0=G2, scalar=V1, in1=desc[:, :], op0=ALU.is_equal,
                                                    op1=ALU.mult))
                gate(b, 9, dve.tensor_reduce(R2, M2, AX_X, ALU.max))
                gate(b, 10, dve.tensor_scalar(OH2, desc[:, :], R2, None, ALU.is_equal))
                gate(b, 11, dve.tensor_tensor(DL, V1, V0, ALU.subtract))

            def gates_b(b):
                dve.wait_ge(d1["exp"], b + 1)
                gate(b, 12, dve.tensor_scalar(DEN, ex[:, :], 1.0, None, ALU.add))
                gate(b, 13, dve.reciprocal(G1, DEN))
                gate(b, 14, dve.tensor_tensor(G2W, G1, ex[:, :], ALU.mult))
                gate(b, 15, dve.tensor_scalar(C1, OH1, G1, None, ALU.mult))
                gate(b, 16, dve.scalar_tensor_tensor(out=C, in0=OH2, scalar=G2W, in1=C1, op0=ALU.mult,
                                                     op1=ALU.add))

            def hand_over(b):
                dve.wait_ge(d1["b2"], b + 1)
                wait(dve, d1["o"], EXPERTS * b)
                dve.tensor_tensor(first_o, x3, ps_m[:, D:2 * D], ALU.add).then_inc(d1["o0"], 1)
                dve.tensor_copy(gates, C).then_inc(d1["gates"], 1)

            def add_expert(b, e):
                if e == 0:
                    dve.wait_ge(d1["o0"], b + 1)
                    dve.wait_ge(d1["gates"], b + 1)
                    wait(dve, d1["out"], 16 * b)
                dve.wait_ge(d1["y"], EXPERTS * b + e + 1)
                wait(dve, d1["o"], EXPERTS * b + e)
                dve.scalar_tensor_tensor(out=o, in0=ps_y2[e % 2][:, 0:D], scalar=gates[:, e:e + 1],
                                         in1=first_o if e == 0 else o, op0=ALU.mult,
                                         op1=ALU.add).then_inc(d1["o"], 1)

            def prepare_records(i, s):
                wait(dve, b_in[s], 16 * (i + 1))
                if not isinstance(i, int) or i > 0:
                    dve.wait_ge(b_mm, 2 * BSLOTS * (i - 1) + 2 * s + 2)
                for t in range(BG):
                    ins = dve.tensor_scalar(bonehot[:, s, t, :], iota_w[:, :], rec_in[:, s, t, 1:2].bitcast(F32),
                                            rec_in[:, s, t, 2:3].bitcast(F32), ALU.is_equal, ALU.mult)
                ins.then_inc(b_oh[s], 1)

            regs = [dve.alloc_register(f"window{t}") for t in range(UTILES)]

            def add_tiles(i, u):
                m = STEP_TILES * i + UTILES * u
                dve.load(regs, window_of[0:1, bass.ds(m, UTILES)])
                starts = [dve.snap(r, min_val=0, max_val=NPAD - WIN) for r in regs]
                dve.wait_ge(b_mm, UNITS * i + u + 1)
                for t in range(UTILES):
                    wait(dve, b_add, m + t)
                    cols = acc[:, :, bass.ds(starts[t], WIN)]
                    dve.tensor_tensor(cols, cols, ps_seg[u % 2][:, t * KD * WIN:(t + 1) * KD * WIN]
                                      .rearrange("p (k w) -> p k w", k=KD), ALU.add).then_inc(b_add, 1)

            def step1(i, tiles, node, expert):
                if node is not None and tiles:
                    dve.wait_ge(b_add, STEP_TILES * i)
                for e in range(UNITS):
                    if node is not None:
                        node_work(node, e)
                    if tiles:
                        add_tiles(i, e)
                        if e % 2:
                            prepare_records(i + 1, e // 2)
                    if expert is not None and e >= 1:
                        add_expert(expert, e - 1)
                if expert is not None:
                    add_expert(expert, EXPERTS - 1)
                if node is not None:
                    hand_over(node)

            dve.wait_ge(c_wback, 16)
            for s in range(BSLOTS):
                prepare_records(0, s)
            both_ways1(dve, early_flag1(dve), step1)

        @block.scalar
        def _(act):
            def std_a(b):
                act.wait_ge(a_mv, b + 1)
                hold(act)
                act.activation(std[:, 0:1], mv[:, 0, 1:2], ACT.Sqrt, bias=eps_c[:, 0:1]).then_inc(a_std, 1)

            def copy_hT(b, q):
                act.wait_ge(a_tr, b + 1)
                wait(act, a_ch, T_CHUNKS * (b - 1))
                hold(act)
                act.activation(hT[:, q, :], ps_t[:, 0:D], ACT.Copy).then_inc(a_hT, 1)

            def evict(b, q, times):
                for c in range(1, T_CHUNKS, 2):
                    act.wait_ge(a_ch, T_CHUNKS * b + c + 1)
                    if c == 1:
                        wait(act, a_out[q], 16 * times)
                    hold(act)
                    act.activation(tbuf[q][:, c * CH:(c + 1) * CH], t_banks[c % 4][:, :],
                                   ACT.Copy).then_inc(a_ev_s, 1)
                act.wait_ge(a_ev_v, 4 * b + 4 + 2)
                act.wait_ge(a_ev_s, 4 * b + 4 + 2)
                act.dma_start(table0_rows[bass.ds(b * P, P), :], tbuf[q]).then_inc(a_out[q], 16)

            act.wait_ge(s_kv, 3)
            std_a(0)
            copy_hT(0, 0)
            std_a(1)
            copy_hT(1, 1)
            evict(0, 0, 0)
            std_a(2)
            copy_hT(2, 0)
            evict(1, 1, 0)
            with act.Fori(1, BLOCKS // 2) as j:
                std_a(2 * j + 1)
                copy_hT(2 * j + 1, 1)
                evict(2 * j, 0, j)
                std_a(2 * j + 2)
                copy_hT(2 * j + 2, 0)
                evict(2 * j + 1, 1, j)
            evict(BLOCKS - 1, 0, BLOCKS // 2)
            act.wait_ge(s_c, 16 * N_CONSTS)

            def block_std(v, b):
                act.wait_ge(v["mv"], b + 1)
                hold(act)
                act.activation(std[:, 0:1], mv[:, 0, 1:2], ACT.Sqrt, bias=eps_c[:, 0:1]).then_inc(v["std"], 1)

            def block0(b):
                block_std(d0, b)
                act.wait_ge(d0["trH"], b + 1)
                wait(act, d0["hid"], 2 * b)
                hold(act)
                act.activation(hT[:, 0, :], ps_t[:, D:2 * D], ACT.Copy).then_inc(d0["hT"], 1)
                wait(act, d0["y"], b)
                for q in range(2):
                    act.wait_ge(d0["hid"], 2 * b + q + 1)
                    hold(act)
                    for c in range(4 * q, 4 * q + 4):
                        act.activation(hid[:, c * P:(c + 1) * P], ps_h[q][:, (c % 4) * P:(c % 4 + 1) * P],
                                       ACT.Gelu_apprx_tanh, bias=b1_sb[:, c:c + 1]).then_inc(d0["gelu"], 1)
                act.wait_ge(d0["base"], b + 1)
                act.dma_start(base_d[bass.ds(b * P, P), :], base[:, :]).then_inc(d0["out"], 16)

            def step1(i, tiles, node, expert):
                if expert is not None:
                    act.wait_ge(d1["hT"], expert + 1)
                    wait(act, d1["hid"], EXPERTS * expert)
                    hold(act)
                    act.activation(hT[:, 0, :], hT[:, 1, :], ACT.Copy).then_inc(d1["hT2"], 1)
                for e in range(UNITS):
                    if expert is not None:
                        relu(expert, e)
                    if node is not None:
                        node_work(node, e)
                if expert is not None:
                    act.wait_ge(d1["o"], EXPERTS * (expert + 1))
                    act.dma_start(out[bass.ds(expert * P, P), :], o).then_inc(d1["out"], 16)

            def node_work(b, e):
                if e == 2:
                    block_std(d1, b)
                if e == 4:
                    act.wait_ge(d1["trH"], b + 1)
                    wait(act, d1["hT2"], b)
                    wait(act, d1["lg"], b)
                    hold(act)
                    act.activation(hT[:, 1, :], ps_t[:, D:2 * D], ACT.Copy).then_inc(d1["hT"], 1)
                if e == 5:
                    act.wait_ge(d1["gate"], GATE_STEPS * b + 11)
                    hold(act)
                    act.activation(ex[:, :], gs[:, 4:5], ACT.Exp).then_inc(d1["exp"], 1)

            def relu(b, e):
                act.wait_ge(d1["hid"], EXPERTS * b + e + 1)
                wait(act, d1["y"], EXPERTS * b + max(e - 1, 0))
                hold(act)
                for c in range(EC):
                    ins = act.activation(hid[:, (e % 2) * EHID + c * P:(e % 2) * EHID + (c + 1) * P],
                                         ps_h[e % 2][:, c * P:(c + 1) * P], ACT.Relu,
                                         bias=eb1_sb[:, e * EC + c:e * EC + c + 1])
                ins.then_inc(d1["relu"], 1)

            block0(0)
            with act.Fori(1, BLOCKS) as b:
                block0(b)
            for t in range(BATCHES):
                act.wait_ge(m_mv, MB * (t + 1))
                act.activation(std[:, :], mv[:, :, 1], ACT.Sqrt, bias=eps_c[:, 0:1]).then_inc(m_std, 1)
            step1(None, False, 0, None)
            step1(None, False, 1, 0)
            with act.Fori(2, BLOCKS) as b:
                step1(None, False, b, b - 1)
            step1(None, False, None, BLOCKS - 1)

        @block.tensor
        def _(pe):
            pe.wait_ge(s_k, 12)
            pe.wait_ge(s_kv, 3)

            def transpose_block(src, dst, done):
                for k in range(KD):
                    ins = pe.transpose(dst[:, k * P:(k + 1) * P], src[:, k * P:(k + 1) * P], ident[:, :])
                ins.then_inc(done, 1)

            def count_pass(i, first, last):
                for k, (t0, n) in enumerate(SPLITS):
                    pe.wait_ge(c_ob1, NSPLIT * i + k + 1)
                    pe.matmul(ps_count[:, 0:n * WINDOWS], ones_bf[:, :],
                              inb[:, t0:t0 + n, :].rearrange("p t b -> p (t b)"),
                              start=(first and k == 0), stop=(last and k == NSPLIT - 1)).then_inc(c_mm1, 1)

            count_pass(0, True, False)
            with pe.Fori(1, BLOCKS - 1) as i:
                count_pass(i, False, False)
            count_pass(BLOCKS - 1, False, True)
            for r in range(4):
                pe.wait_ge(c_cmp, r + 1)
                wait(pe, c_win, r)
                pe.matmul(ps_count[:, 0:BTILES // 4], ones_bf[0:WINDOWS, :],
                          inb[:, :, :].rearrange("p t b -> p (t b)")[0:WINDOWS, 0:BTILES // 4],
                          start=True, stop=True).then_inc(c_mm1, 1)

            def transpose_a(b):
                pe.wait_ge(a_h, b + 1)
                wait(pe, a_hT, b)
                transpose_block(h, ps_t, a_tr)

            def rank_split(i, k):
                t0, n = SPLITS[k]
                pe.wait_ge(c_ob, NSPLIT * i + k + 1)
                wait(pe, c_take, 3 * (NSPLIT * i + k))

                def tiles(a, b):
                    return inb[:, t0 + a:t0 + b, :].rearrange("p t b -> p (t b)")

                for d in range(1, n):
                    pe.matmul(ps_place[:, d * WINDOWS:n * WINDOWS], ones_bf[:, :], tiles(0, n - d),
                              start=(d == 1), stop=False, skip_group_check=True)
                pe.matmul(ps_place[:, 0:n * WINDOWS], before_bf[:, :], tiles(0, n), start=False, stop=True,
                          skip_group_check=True)
                for t in range(n):
                    ins = pe.matmul(ps_tot[:, 0:WINDOWS], ones_bf[:, :], tiles(t, t + 1), start=(t == 0),
                                    stop=(t == n - 1))
                ins.then_inc(c_mm, 1)

            def table_and_ranks(b, q):
                pe.wait_ge(a_hT, b + 1)
                for c in range(T_CHUNKS):
                    pe.wait_ge((a_ev_v, a_ev_s)[c % 2], 4 * b + c // 2 + 1)
                    for k in range(KD):
                        ins = pe.matmul(t_banks[c % 4][:, :], hT[:, q, k * P:(k + 1) * P],
                                        wrel_sb[:, k, c * CH:(c + 1) * CH], start=(k == 0), stop=(k == KD - 1))
                    ins.then_inc(a_ch, 1)
                    if c < NSPLIT:
                        rank_split(b, c)

            transpose_a(0)
            pe.wait_ge(s_w, 32)
            transpose_a(1)
            table_and_ranks(0, 0)
            transpose_a(2)
            table_and_ranks(1, 1)
            with pe.Fori(1, BLOCKS // 2) as j:
                transpose_a(2 * j + 1)
                table_and_ranks(2 * j, 0)
                transpose_a(2 * j + 2)
                table_and_ranks(2 * j + 1, 1)
            table_and_ranks(BLOCKS - 1, 0)
            pe.wait_ge(c_take, 3 * NSPLIT * BLOCKS)
            pe.wait_ge(a_ev_v, 4 * BLOCKS + 2)
            pe.wait_ge(a_ev_s, 4 * BLOCKS + 2)
            pe.wait_ge(s_c, 16 * N_CONSTS)

            def sum_window(s, done):
                for k in range(KD):
                    for t in range(TG):
                        ins = pe.matmul(ps_seg[s][:, k * WIN:(k + 1) * WIN], ring[:, s, t, k * P:(k + 1) * P],
                                        onehot[:, s, t, :], start=(t == 0), stop=(t == TG - 1))
                ins.then_inc(done, 1)

            def group(i):
                for s in range(SLOTS):
                    pe.wait_ge(l0["rows"][s], 16 * TG * (i + 1))
                    pe.wait_ge(l0["oh"][s], i + 1)
                    wait(pe, l0["acc"][s], i)
                    sum_window(s, l0["mm"][s])

            def all_windows():
                with pe.Fori(0, GROUPS) as g:
                    pe.wait_ge(l0["rows"][0], 16 * TG * (g + 1))
                    hold(pe)
                    with pe.Fori(0, WINDOWS) as w:
                        pe.wait_ge(l0["goh"], g * WINDOWS + w + 1)
                        pe.wait_ge(l0["gacc"], g * WINDOWS + w + 1)
                        sum_window(0, l0["gmm"])

            def block0(b):
                pe.wait_ge(d0["accs"], b + 1)
                wait(pe, d0["w"], b)
                transpose_block(accs, ps_t[:, 0:D], d0["trA"])
                pe.wait_ge(d0["h"], b + 1)
                wait(pe, d0["hT"], b)
                transpose_block(h, ps_t[:, D:2 * D], d0["trH"])
                pe.wait_ge(d0["hT"], b + 1)
                for k in range(KD):
                    ins = pe.matmul(ps_m[:, 0:1], hT[:, 0, k * P:(k + 1) * P], wr_sb[:, k:k + 1],
                                    start=(k == 0), stop=(k == KD - 1))
                ins.then_inc(d0["rt"], 1)
                wait(pe, d0["gelu"], HC * b)
                for q in range(2):
                    for c in range(4 * q, 4 * q + 4):
                        for k in range(KD):
                            ins = pe.matmul(ps_h[q][:, (c % 4) * P:(c % 4 + 1) * P],
                                            w1_sb[:, k, c * P:(c + 1) * P], hT[:, 0, k * P:(k + 1) * P],
                                            start=(k == 0), stop=(k == KD - 1))
                    ins.then_inc(d0["hid"], 1)
                wait(pe, d0["y1"], b)
                for c in range(HC):
                    pe.wait_ge(d0["gelu"], HC * b + c + 1)
                    ins = pe.matmul(ps_y[:, 0:D], hid[:, c * P:(c + 1) * P], w2_sb[:, c, :],
                                    start=(c == 0), stop=(c == HC - 1))
                ins.then_inc(d0["y"], 1)

            def node_work(b, e):
                if e == 0:
                    pe.wait_ge(d1["h_in"], 16 * (b + 1))
                    wait(pe, d1["o0"], b)
                    transpose_block(hin, ps_t[:, 0:D], d1["tr1"])
                if e == 2:
                    pe.wait_ge(d1["mul"], b + 1)
                    wait(pe, d1["z"], b)
                    for a, left in enumerate((addT, mulT)):
                        for k in range(KD):
                            ins = pe.matmul(ps_g[:, a * D:(a + 1) * D], left[:, k * P:(k + 1) * P],
                                            gw_sb[:, a, k, :], start=(k == 0), stop=(k == KD - 1))
                    ins.then_inc(d1["g"], 1)
                if e == 4:
                    pe.wait_ge(d1["h"], b + 1)
                    transpose_block(h, ps_t[:, D:2 * D], d1["trH"])
                if e == 5:
                    pe.wait_ge(d1["hT"], b + 1)
                    for k in range(KD):
                        ins = pe.matmul(ps_m[:, 0:EXPERTS], hT[:, 1, k * P:(k + 1) * P], wg_sb[:, k, :],
                                        start=(k == 0), stop=(k == KD - 1))
                    ins.then_inc(d1["lg"], 1)
                if e == 7:
                    pe.wait_ge(d1["gate"], GATE_STEPS * (b + 1))
                    pe.transpose(ps_m[0:EXPERTS, P:2 * P], g8[:, 7, :], ident[:, :]).then_inc(d1["ct"], 1)

            def hidden(b, e):
                if e == 0:
                    pe.wait_ge(d1["hT2"], b + 1)
                wait(pe, d1["relu"], EXPERTS * b + max(e - 1, 0))
                for c in range(EC):
                    for k in range(KD):
                        ins = pe.matmul(ps_h[e % 2][:, c * P:(c + 1) * P],
                                        ew1_sb[:, e, k, c * P:(c + 1) * P], hT[:, 0, k * P:(k + 1) * P],
                                        start=(k == 0), stop=(k == KD - 1))
                ins.then_inc(d1["hid"], 1)

            def outputs(b, e):
                pe.wait_ge(d1["relu"], EXPERTS * b + e + 1)
                wait(pe, d1["o"], EXPERTS * b + max(e - 1, 0))
                for c in range(EC):
                    ins = pe.matmul(ps_y2[e % 2][:, 0:D],
                                    hid[:, (e % 2) * EHID + c * P:(e % 2) * EHID + (c + 1) * P],
                                    ew2_sb[:, e, c, :], start=(c == 0), stop=(c == EC - 1))
                ins.then_inc(d1["y"], 1)

            def unit(i, u):
                s = u // 2
                if u % 2 == 0:
                    pe.wait_ge(b_rows[s], 16 * BG * (i + 1))
                    pe.wait_ge(b_oh[s], i + 1)
                if not isinstance(i, int) or UNITS * i + u >= 2:
                    pe.wait_ge(b_add, STEP_TILES * i + UTILES * (u - 1))
                for t in range(UTILES):
                    j = u % 2 * UTILES + t
                    for k in range(KD):
                        ins = pe.matmul(ps_seg[u % 2][:, (t * KD + k) * WIN:(t * KD + k + 1) * WIN],
                                        bring[:, s, j, k * P:(k + 1) * P], bonehot[:, s, j, :],
                                        start=True, stop=True)
                ins.then_inc(b_mm, 1)

            def step1(i, tiles, node, expert):
                for e in range(UNITS):
                    if expert is not None:
                        hidden(expert, e)
                    if node is not None:
                        node_work(node, e)
                    if tiles:
                        unit(i, e)
                    if expert is not None and e >= 1:
                        outputs(expert, e - 1)
                if node is not None:
                    pe.wait_ge(d1["cts"], node + 1)
                    pe.matmul(ps_m[:, D:2 * D], cTs[:, :], eb2_sb[:, :], start=True, stop=True).then_inc(d1["b2"], 1)
                if expert is not None:
                    outputs(expert, EXPERTS - 1)

            both_ways0(pe, early_flag0(pe), group, all_windows, block0)

            step = [9]
            done = 0
            for half in range(2):
                step[0] += 1
                for k in range(16):
                    step[0] += 2
                    pe.wait_ge(q_v, step[0])
                    pe.matmul(ps_m[:, 0:1], ones[:, :], cnt[:, :], start=True, stop=True).then_inc(q_mm, 1)
                    step[0] += 3
                step[0] += 4 if half == 0 else 2
            pe.wait_ge(q_v, step[0])
            pe.matmul(ps_m[:, 0:1], ones[:, :], cnt[:, :], start=True, stop=True).then_inc(q_mm, 1)
            pe.wait_ge(q_v, step[0] + 2)
            pe.matmul(ps_m[:, P:P + BLOCKS], ones[:, :], kf[:, 3, :], start=True, stop=True)
            pe.matmul(ps_m[:, 2 * P:2 * P + BLOCKS], before[:, :], kf[:, 3, :], start=True,
                      stop=True).then_inc(q_mm, 1)

            pe.wait_ge(s_ew, 32)
            pe.wait_ge(s_kv, 7)

            both_ways1(pe, early_flag1(pe), step1)


def kernel(**inputs):
    import numpy as np
    import concourse.bacc as bacc
    from concourse import mybir as _mybir
    from concourse.bass_utils import run_bass_kernel_spmd

    def a(name):
        return np.ascontiguousarray(inputs[name])

    def padded(v, n, fill):
        return np.concatenate([v, np.full((n - v.shape[0],) + v.shape[1:], fill, v.dtype)])

    def by_group(v, fill):
        return np.ascontiguousarray(padded(v, EPAD, fill).reshape(GROUPS, TG, P).transpose(0, 2, 1))

    def by_lane(v):
        return np.ascontiguousarray(v.transpose(1, 0, 2).reshape(P, LANE_TILES))

    src, rel, dst = (by_group(a(n), f) for n, f in (("src", 0), ("edge_type_16", 0), ("dst", N - 1)))
    arrays = {
        "x": padded(a("x"), NPAD, 0),
        "edge_ints": np.ascontiguousarray(np.concatenate([src, rel, dst], axis=2)),
        "dst_lanes": by_lane(dst), "src_lanes": by_lane(src),
        "norm0": by_group(a("edge_weight1").reshape(E), 0),
        "norm1_lanes": by_lane(by_group(a("edge_weight"), 0)),
        "wrel": np.ascontiguousarray(a("L0_gnn_weight").reshape(RELS, KD, P, D).transpose(1, 2, 0, 3)),
        "wr": np.ascontiguousarray(a("L0_ffn_wr").reshape(KD, P).T),
        "br": a("L0_ffn_br"),
        "w1": a("L0_ffn_w1"), "b1": np.ascontiguousarray(a("L0_ffn_b1").reshape(HC, P).T),
        "w2": a("L0_ffn_w2"), "b2": a("L0_ffn_b2"),
        "gw1t": np.ascontiguousarray(a("L1_gnn_W1").T), "gb1": a("L1_gnn_b1"),
        "gw2t": np.ascontiguousarray(a("L1_gnn_W2").T), "gb2": a("L1_gnn_b2"),
        "wg": a("L1_ffn_Wg"), "bg": a("L1_ffn_bg"), "gbias": a("L1_ffn_bias"),
        "ew1": a("L1_ffn_W1"),
        "eb1": np.ascontiguousarray(a("L1_ffn_b1").reshape(EXPERTS * EC, P).T),
        "ew2": a("L1_ffn_W2"), "eb2": a("L1_ffn_b2"),
    }
    nc = bacc.Bacc("TRN2", target_bir_lowering=False, num_devices=1)
    args = {n: nc.dram_tensor(f"in_{n}", v.shape, _mybir.dt.from_np(v.dtype), kind="ExternalInput").ap()
            for n, v in arrays.items()}
    args["out"] = nc.dram_tensor("out_x", (NPAD, D), _mybir.dt.float32, kind="ExternalOutput").ap()
    gnn_kernel(nc, **args)
    r = run_bass_kernel_spmd(nc, [{f"in_{n}": v for n, v in arrays.items()}], core_ids=[0])
    return r.results[0]["out_x"][:N]
```
